# Optimizing a Trainium2 kernel written in Bass

```python
import numpy as np
import jax
import jax.numpy as jnp

def _softmax(x, axis=-1):
    return jax.nn.softmax(x, axis=axis)

def _gelu(x):
    return jax.nn.gelu(x, approximate=True)

def _silu(x):
    return jax.nn.silu(x)

def _sigmoid(x):
    return jax.nn.sigmoid(x)

def _layernorm(x, axis=-1, eps=1e-05):
    m = jnp.mean(x, axis=axis, keepdims=True)
    v = jnp.var(x, axis=axis, keepdims=True)
    return (x - m) / jnp.sqrt(v + eps)

def _scatter_add(tgt, idx, src, axis=0):
    return tgt.at[idx].add(src)

def _segment_sum(src, seg, n):
    return jax.ops.segment_sum(src, seg, n)
kernel_name = 'mk_sandwich_d1_jaxref_r4_b2c2d7'

def setup_inputs(seed: int=0):
    np.random.seed(seed)
    _w = jnp.asarray

    def _L0_attn_setup():
        import jax, jax.numpy as jnp
        import numpy as np
        import math
        B, T, D = (4, 1024, 512)
        H = 16
        HD = D // H
        L = 64
        K_TOP = 4
        key = jax.random.key(seed)
        ks = jax.random.split(key, 10)
        lim = 1.0 / math.sqrt(D)
        u = lambda k, shape: jax.random.uniform(k, shape, jnp.float32, -lim, lim)
        return {'hidden_states': jax.random.normal(ks[0], (B, T, D), jnp.float32), 'Wq': u(ks[1], (D, D)), 'bq': u(ks[2], (D,)), 'Wk': u(ks[3], (D, D)), 'bk': u(ks[4], (D,)), 'Wv': u(ks[5], (D, D)), 'bv': u(ks[6], (D,)), 'Wo': u(ks[7], (D, D)), 'bo': u(ks[8], (D,)), 'latent_keys': jax.random.normal(ks[9], (L, D), jnp.float32) * 0.1}
    _L0_attn_in = _L0_attn_setup()

    def _L0_ffn_setup():
        import jax, jax.numpy as jnp
        import numpy as np
        D_MODEL = 512
        D_EXPERT = 2048
        EPS = 1e-08

        def ternary_quant(w):
            scale = jnp.mean(jnp.abs(w)) + EPS
            q = jnp.clip(jnp.round(w / scale), -1.0, 1.0) * scale
            return w + jax.lax.stop_gradient(q - w)
        key = jax.random.key(seed)
        k_x, k_up, k_gate, k_down = jax.random.split(key, 4)
        std_in = 1.0 / np.sqrt(D_MODEL)
        std_exp = 1.0 / np.sqrt(D_EXPERT)
        return {'x': jax.random.normal(k_x, (4, 512, D_MODEL), dtype=jnp.float32), 'W_up': jax.random.normal(k_up, (D_EXPERT, D_MODEL), dtype=jnp.float32) * std_in, 'W_gate': jax.random.normal(k_gate, (D_EXPERT, D_MODEL), dtype=jnp.float32) * std_in, 'W_down': jax.random.normal(k_down, (D_MODEL, D_EXPERT), dtype=jnp.float32) * std_exp}
    _L0_ffn_in = _L0_ffn_setup()
    _d = {'L0_attn_hidden_states': _L0_attn_in['hidden_states'], 'L0_attn_Wq': _L0_attn_in['Wq'], 'L0_attn_bq': _L0_attn_in['bq'], 'L0_attn_Wk': _L0_attn_in['Wk'], 'L0_attn_bk': _L0_attn_in['bk'], 'L0_attn_Wv': _L0_attn_in['Wv'], 'L0_attn_bv': _L0_attn_in['bv'], 'L0_attn_Wo': _L0_attn_in['Wo'], 'L0_attn_bo': _L0_attn_in['bo'], 'L0_attn_latent_keys': _L0_attn_in['latent_keys'], 'L0_ffn_W_up': _L0_ffn_in['W_up'], 'L0_ffn_W_gate': _L0_ffn_in['W_gate'], 'L0_ffn_W_down': _L0_ffn_in['W_down']}
    _x0 = _d['L0_attn_hidden_states']
    _d['L0_attn_hidden_states'] = jax.random.normal(jax.random.fold_in(jax.random.key(seed), 1), (2, 2048, 512), dtype=_x0.dtype)
    del _x0
    return _d

def reference(L0_attn_hidden_states, L0_attn_Wq, L0_attn_bq, L0_attn_Wk, L0_attn_bk, L0_attn_Wv, L0_attn_bv, L0_attn_Wo, L0_attn_bo, L0_attn_latent_keys, L0_ffn_W_up, L0_ffn_W_gate, L0_ffn_W_down):

    def _L0_attn_ref(hidden_states, Wq, bq, Wk, bk, Wv, bv, Wo, bo, latent_keys):
        import jax, jax.numpy as jnp
        import numpy as np
        import math
        B, T, D = (4, 1024, 512)
        H = 16
        HD = D // H
        L = 64
        K_TOP = 4
        b, t, d = hidden_states.shape
        Q = (hidden_states @ Wq.T + bq).reshape(b, t, H, HD).transpose(0, 2, 1, 3)
        K = (hidden_states @ Wk.T + bk).reshape(b, t, H, HD).transpose(0, 2, 1, 3)
        V = (hidden_states @ Wv.T + bv).reshape(b, t, H, HD).transpose(0, 2, 1, 3)
        latent = latent_keys.reshape(L, H, HD)
        attn_logits = jnp.einsum('bhtd,lhd->bhtl', Q, latent) / math.sqrt(HD)
        topk_logits, topk_idx = jax.lax.top_k(attn_logits, K_TOP)
        attn_weights = jax.nn.softmax(topk_logits, axis=-1)
        latent_h = latent.transpose(1, 0, 2)
        selected = latent_h[jnp.arange(H)[None, :, None, None], topk_idx]
        weighted = jnp.einsum('bhtk,bhtkd->bhtd', attn_weights, selected)
        attn_output = (weighted + V).transpose(0, 2, 1, 3).reshape(b, t, d)
        return attn_output @ Wo.T + bo

    def _L0_ffn_ref(x, W_up, W_gate, W_down):
        import jax, jax.numpy as jnp
        import numpy as np
        D_MODEL = 512
        D_EXPERT = 2048
        EPS = 1e-08

        def ternary_quant(w):
            scale = jnp.mean(jnp.abs(w)) + EPS
            q = jnp.clip(jnp.round(w / scale), -1.0, 1.0) * scale
            return w + jax.lax.stop_gradient(q - w)
        wu = ternary_quant(W_up)
        wg = ternary_quant(W_gate)
        wd = ternary_quant(W_down)
        up = jnp.einsum('bsd,ed->bse', x, wu)
        gate = jnp.einsum('bsd,ed->bse', x, wg)
        hidden = jax.nn.silu(up) * gate
        return jnp.einsum('bse,de->bsd', hidden, wd)
    x = L0_attn_hidden_states
    x = x + _layernorm(_L0_attn_ref(_layernorm(x, axis=-1), L0_attn_Wq, L0_attn_bq, L0_attn_Wk, L0_attn_bk, L0_attn_Wv, L0_attn_bv, L0_attn_Wo, L0_attn_bo, L0_attn_latent_keys), axis=-1)
    x = x + _layernorm(_L0_ffn_ref(_layernorm(x, axis=-1), L0_ffn_W_up, L0_ffn_W_gate, L0_ffn_W_down), axis=-1)
    return x

_drawn_inputs = setup_inputs


def setup_inputs(seed=0):
    import zlib

    import numpy as np

    out = dict(_drawn_inputs(seed))
    spreads = {}
    factors = {'L0_attn_bq': 3.303}
    for name, (base, spread) in spreads.items():
        noise = np.random.default_rng([zlib.crc32(name.encode()), seed]).standard_normal(out[name].shape)
        drawn = base * np.exp(spread * noise) if base else spread * noise
        out[name] = jnp.asarray(drawn.astype(out[name].dtype))
    for name, factor in factors.items():
        out[name] = (out[name] * factor).astype(out[name].dtype)
    return out
```

```python
from contextlib import ExitStack

import concourse.bass as bass
from concourse import mybir

ALU = mybir.AluOpType
ACT = mybir.ActivationFunctionType
AX = mybir.AxisListType
F32 = mybir.dt.float32
F16 = mybir.dt.float16
U32 = mybir.dt.uint32
RMAX = bass.bass_isa.ReduceOp.max
RADD = bass.bass_isa.ReduceOp.add

P = 128
D = 512
KD = D // P
H = 16
HD = D // H
NL = 64
TOPK = 4
E = 2048
NE = E // P
TT = 4
CH = TT * P
PADS = 8 - TOPK
LW = NL + PADS
EPS = 1e-5
QEPS = 1e-8

PAD = -3.0e38
HIT = -1.0e30
XS = 2.0 ** 11
WS = 2.0 ** 13
AS = 2.0 ** 5
PROJ = AS / (XS * WS)
PS = 2.0 ** 11
HS = 2.0 ** -26
TINY = 2.0 ** -100

KINDS = ("S1", "Q", "T2", "L", "PT", "DN", "VW", "WO")


def pe_order(att, ffn, nxt):
    o = []
    if att:
        o += [("Q", 0, m) for m in range(KD)]
    if ffn:
        o += [("T2", -1, t) for t in range(TT)]
    if att:
        o += [("L", 0, n) for n in range(4)]
        for t in range(TT - 1):
            o += [("PT", 0, 2 * t), ("PT", 0, 2 * t + 1)]
            if t < 2:
                o += [("L", 0, 2 * t + 4), ("L", 0, 2 * t + 5)]
    if ffn:
        o += [("DN", -1, 0)]
    if att:
        o += [("PT", 0, 6), ("PT", 0, 7)]
    if ffn:
        o += [("DN", -1, 1)]
    if att:
        o += [("VW", 0, m) for m in range(KD)]
    if ffn:
        o += [("DN", -1, 2), ("DN", -1, 3)]
    if nxt:
        o += [("S1", 1, t) for t in range(TT)]
    if att:
        o += [("WO", 0, t) for t in range(TT)]
    return o


def ring_plan(att, ffn, nxt, before):
    seq = list(before) + pe_order(att, ffn, nxt)
    return {seq[n]: (n % 4, seq[n - 4]) for n in range(4, len(seq))}


def build(nc, x, Wq, bq, Wv, bv, Wo, bo, lat, Wu, Wg, Wd, out):
    NCH = x.shape[0] * x.shape[1] // CH
    with ExitStack() as ctx:
        def sb(name, shape, dt=F32):
            return ctx.enter_context(nc.sbuf_tensor(name, shape, dt))

        def sem(name):
            return ctx.enter_context(nc.semaphore(name))

        TU = sb("TU", [P, KD * E], F16)
        TG = sb("TG", [P, KD * E], F16)
        TD = sb("TD", [P, NE * D], F16)
        tu = TU[:, :].rearrange("p (k e) -> p k e", k=KD)
        tg = TG[:, :].rearrange("p (k e) -> p k e", k=KD)
        td = TD[:, :].rearrange("p (j d) -> p j d", j=NE)
        wT = [[sb(f"w{w}_{s}", [P, KD, D], F16) for s in ("hi", "lo")] for w in ("q", "v", "o")]
        latL = [sb(f"latL_{s}", [P, KD, 4 * NL], F16) for s in ("hi", "lo")]
        latV = [sb(f"latV_{s}", [P, H // 2, 2 * HD], F16) for s in ("hi", "lo")]
        bo_b = sb("bo_b", [P, D])
        id32 = sb("id32", [P, P])
        id16 = sb("id16", [P, P], F16)

        x_in = sb("x_in", [P, TT, D])
        x1 = sb("x1", [P, TT, D])
        xT = [sb(f"xT_{s}", [P, KD, CH], F16) for s in ("hi", "lo")]
        qaT = [sb(f"qaT_{s}", [P, KD, CH], F16) for s in ("hi", "lo")]
        Lb = sb("Lb", [P, 2, H, LW])
        Lr = sb("Lr", [P, H, LW])
        PT = sb("PT", [P, 2, 8, CH], F16)
        X1T = sb("X1T", [P, 2, KD, CH], F16)
        hT = sb("hT", [P, 2, NE, CH], F16)
        ugt = sb("ugt", [P, 4, CH])
        p32 = sb("p32", [P, 2, CH])
        Pb = p32[:, :, :].rearrange("p a b -> p (a b)")
        row = sb("row", [P, 2, D])
        xn = sb("xn", [P, 2, D])

        mv1 = sb("mv1", [P, TT, 2])
        st1 = sb("st1", [P, TT, 6])
        sty = sb("sty", [P, 2, 6])
        mvy = sb("mvy", [P, 2, 2])
        stx = sb("stx", [P, 2, 6])
        mvx = sb("mvx", [P, 2, 2])
        stf = sb("stf", [P, 2, 6])
        mvf = sb("mvf", [P, 2, 2])
        va1 = sb("va1", [P, TT])
        vay = sb("vay", [P, 2])
        vax = sb("vax", [P, 2])
        vaf = sb("vaf", [P, 2])
        rs1 = sb("rs1", [P, TT])
        rsy = sb("rsy", [P, 2])
        rsx = sb("rsx", [P, 2])
        rsf = sb("rsf", [P, 2])
        rcf = sb("rcf", [P, 2])
        nh = sb("nh", [P, TT])
        v8 = sb("v8", [P, 2, H, 8])
        d4 = sb("d4", [P, 2, H, TOPK])
        s4 = sb("s4", [P, 2, H])
        r4 = sb("r4", [P, 2, H])
        bqc = sb("bqc", [P, KD])
        bvc = sb("bvc", [P, KD])
        bqs = sb("bqs", [P, KD])
        bvs = sb("bvs", [P, KD])
        mx = sb("mx", [P, 6])
        mg = sb("mg", [P, 4])
        ma = sb("ma", [P, 4])
        sc = sb("sc", [P, 4])
        inv = sb("inv", [P, 4])
        up = sb("upw", [P, 4])
        upb = sb("upb", [P, 2])
        clo = sb("clo", [P, 2])
        asum = sb("asum", [P, 24])
        tot = sb("tot", [P, 3])
        tota = sb("tota", [P, 3])
        sw = sb("sw", [P, 3])
        hw = sb("hw", [P, 3])
        nhw = sb("nhw", [P, 3])
        cu = sb("cu", [P, 1])
        cf = sb("cf", [P, 2])

        ug = ctx.enter_context(nc.psum_tensor("ug", [P, 4, CH], F32))
        ring = ctx.enter_context(nc.psum_tensor("ring", [P, 4, CH], F32))

        PER = {}

        def csem(name, n):
            PER[name] = n
            return sem(name)

        x_in_loaded = csem("x_in_loaded", 16)
        x_res_loaded = [sem(f"x_res_loaded{t}") for t in range(TT)]
        out_stored = [sem(f"out_stored{s}") for s in range(2)]
        ln1_stats, ln1_mean, ln1_var, ln1_rstd = (sem(f"ln1_{n}") for n in ("stats", "mean", "var", "rstd"))
        xn1_ready = sem("xn1_ready")
        s1_done, x_hi, x_lo = sem("s1_done"), sem("x_hi"), sem("x_lo")
        q_done, q32_ready, q_hi, q_lo = sem("q_done"), sem("q32_ready"), sem("q_hi"), sem("q_lo")
        l_done, l_ready = sem("l_done"), sem("l_ready")
        top8, v8_ready, d4_ready, e4_ready = sem("top8"), sem("v8_ready"), sem("d4_ready"), sem("e4_ready")
        sum_ready, recip_ready = sem("sum_ready"), sem("recip_ready")
        replaced, shifted, e_ready = sem("replaced"), sem("shifted"), sem("e_ready")
        p_raw, p_ready = sem("p_raw"), sem("p_ready")
        pt_done, pt_hi, pt_lo = sem("pt_done"), sem("pt_hi"), sem("pt_lo")
        vw_done, a32_ready, a_hi, a_lo = sem("vw_done"), sem("a32_ready"), sem("a_hi"), sem("a_lo")
        wo_done, y_ready = sem("wo_done"), sem("y_ready")
        y_stats, y_mean, y_var, y_rstd, z_ready = (sem(f"y_{n}") for n in ("stats", "mean", "var", "rstd", "norm"))
        x1_ready = sem("x1_ready")
        ln2_stats, ln2_mean, ln2_var, ln2_rstd = (sem(f"ln2_{n}") for n in ("stats", "mean", "var", "rstd"))
        xn2_ready = sem("xn2_ready")
        t2_done, x1_hi, x1_lo = sem("t2_done"), sem("x1_hi"), sem("x1_lo")
        ug_done, tanh_ready, t1_ready, h32_ready = sem("ug_done"), sem("tanh_ready"), sem("t1_ready"), sem("h32_ready")
        h_hi, h_lo = sem("h_hi"), sem("h_lo")
        dn_done = sem("dn_done")
        f_stats, f_mean, f_var, f_rstd, f_scale, f_norm = (sem(f"f_{n}") for n in ("stats", "mean", "var", "rstd", "scale", "norm"))
        f_varc = sem("f_varc")
        out_ready = sem("out_ready")
        own_wait = sem("own_wait")
        aw_loaded = [sem(f"aw_loaded{n}") for n in range(7)]
        w_loaded = [sem(f"w_loaded{n}") for n in range(24)]
        zeroed, id_zeroed, consts, idents = sem("zeroed"), sem("id_zeroed"), sem("consts"), sem("idents")
        mx_ready, mg_ready, ma_ready, sc_step, scales = (sem(n) for n in ("mx_ready", "mg_ready", "ma_ready", "sc_step", "scales"))
        wt_done, wt_hi, wt_lo = sem("wt_done"), sem("wt_hi"), sem("wt_lo")
        lat_done, lat_hi, lat_lo = sem("lat_done"), sem("lat_hi"), sem("lat_lo")
        asum_done, tot_ready, tota_ready, tern_step = (sem(n) for n in ("asum_done", "tot_ready", "tota_ready", "tern_step"))
        tern_scale = sem("tern_scale")
        below, tern_ready, tp_done, tp_evicted = (sem(n) for n in ("below", "tern_ready", "tp_done", "tp_evicted"))

        FREED = {"S1": (x_lo, TT), "Q": (q32_ready, KD), "T2": (x1_lo, TT), "L": (l_ready, 8), "PT": (pt_lo, 8),
                 "DN": (f_norm, TT), "VW": (a32_ready, KD), "WO": (y_ready, TT)}

        def wait(eng, s, c, per, n):
            v = c * per + max(n, 0)
            if not isinstance(v, int) or v > 0:
                eng.wait_ge(s, v)

        hT32 = hT[:, :, :, :].rearrange("p s e t -> p (s e t)").bitcast(F32)
        td32 = TD[:, :].bitcast(F32)
        x1t32 = X1T[:, :, :, :].rearrange("p s k t -> p (s k t)").bitcast(F32)
        ugt32 = ugt[:, :, :].rearrange("p a b -> p (a b)")
        pt32 = PT[:, :, :, :].rearrange("p s b t -> p (s b t)").bitcast(F32)
        raw_a = [pt32[:, 0:2048], pt32[:, 2048:4096], x1[:, :, :].rearrange("p t d -> p (t d)")]
        latr = row[:, 0, :]
        stage_hT = [hT32[:, 1024 * q:1024 * q + 1024] for q in range(8)]
        stage_mix = ([td32[:, 1024 * q:1024 * q + 1024] for q in range(4)]
                     + [x1t32[:, 1024 * q:1024 * q + 1024] for q in range(2)]
                     + [ugt32[:, 1024 * q:1024 * q + 1024] for q in range(2)])
        stages = [stage_hT, stage_mix, stage_hT]
        row16 = row[:, :, :].rearrange("p a b -> p (a b)").bitcast(F16)
        tern = [row16[:, 1024 * s:1024 * s + 1024] for s in range(2)]
        belowb = Lr[:, :, :].rearrange("p a b -> p (a b)").bitcast(F16)[:, 0:1024]
        tpb = [ug[:, s, :].bitcast(F16) for s in range(2)]
        junk = ug[:, 2:4, :].rearrange("p a b -> p (a b)")

        xv = x.rearrange("b (c p t) d -> (b c) p t d", p=P, t=TT)
        ov = out.rearrange("b (c p t) d -> (b c) p t d", p=P, t=TT)

        def chunk(v, c):
            return v[c] if isinstance(c, int) else v[bass.ds(c, 1)].rearrange("a p t d -> (a p) t d")

        plans = {
            "first": ring_plan(True, False, True, [("S1", 0, t) for t in range(TT)]),
            "mid": ring_plan(True, True, True, [("WO", -1, t) for t in range(TT)]),
            "last": ring_plan(True, True, False, [("WO", -1, t) for t in range(TT)]),
            "tail": ring_plan(False, True, False, [("WO", -1, t) for t in range(TT)]),
        }

        def bodies(eng, body):
            body(0, "first", True, False, True)
            with eng.Fori(1, NCH - 1) as i:
                body(i, "mid", True, True, True)
            body(NCH - 1, "last", True, True, False)
            body(NCH, "tail", False, True, False)

        block = ctx.enter_context(nc.Block())

        @block.sync
        def _(sp):
            sp.dma_start(raw_a[0].rearrange("p (m d) -> p m d", m=KD), Wq.rearrange("(m p) d -> p m d", p=P)).then_inc(aw_loaded[0], 16)
            sp.dma_start(x_in[:, :, :], xv[0]).then_inc(x_in_loaded, 16)
            for s in range(2):
                sp.dma_start(latr[NL * s:NL * s + NL, :], lat).then_inc(aw_loaded[3], 16)
            sp.dma_start(bqc[:, :], bq.rearrange("(m p) -> p m", p=P), allow_slow_non_contiguous=True).then_inc(aw_loaded[4], 16)
            sp.dma_start(bvc[:, :], bv.rearrange("(m p) -> p m", p=P), allow_slow_non_contiguous=True).then_inc(aw_loaded[5], 16)
            sp.dma_start(raw_a[1].rearrange("p (m d) -> p m d", m=KD), Wv.rearrange("(m p) d -> p m d", p=P)).then_inc(aw_loaded[1], 16)
            sp.dma_start(raw_a[2].rearrange("p (m d) -> p m d", m=KD), Wo.rearrange("(m p) d -> p m d", p=P)).then_inc(aw_loaded[2], 16)
            sp.dma_start(bo_b[:, :], bo.rearrange("(a d) -> a d", a=1).broadcast_to([P, D])).then_inc(aw_loaded[6], 16)
            for w, W in enumerate((Wu, Wg)):
                v = W.rearrange("(q r p) d -> q p r d", p=P, r=2)
                for q in range(8):
                    sp.dma_start(stages[w][q].rearrange("p (r d) -> p r d", r=2), v[q]).then_inc(w_loaded[8 * w + q], 16)
            sp.wait_ge(wt_lo, 12)
            for t in range(TT):
                sp.dma_start(x1[:, t, :], xv[0, :, t, :]).then_inc(x_res_loaded[t], 16)
            v = Wd.rearrange("(a p) (b e) -> a b p e", p=P, b=2)
            for q in range(8):
                sp.wait_ge(tern_ready, q + 1)
                sp.dma_start(stages[2][q], v[q // 2, q % 2]).then_inc(w_loaded[16 + q], 16)

            def body(i, kind, att, ffn, nxt):
                if nxt:
                    wait(sp, xn1_ready, i, TT, TT)
                    sp.dma_start(x_in[:, :, :], chunk(xv, i + 1)).then_inc(x_in_loaded, 16)
                if ffn:
                    for t in range(TT):
                        wait(sp, out_ready, i - 1, TT, t + 1)
                        sp.dma_start(chunk(ov, i - 1)[:, t, :], row[:, t % 2, :]).then_inc(out_stored[t % 2], 16)
                        if att:
                            sp.dma_start(x1[:, t, :], chunk(xv, i)[:, t, :]).then_inc(x_res_loaded[t], 16)

            bodies(sp, body)
            for s in range(2):
                sp.wait_ge(out_stored[s], 32 * NCH)

        @block.tensor
        def _(pe):
            pe.wait_ge(idents, 2)
            for w in range(3):
                pe.wait_ge(aw_loaded[w], 16)
                for m in range(KD):
                    n = KD * w + m
                    if n >= 4:
                        pe.wait_ge(wt_lo, n - 3)
                    for k in range(KD):
                        last = pe.transpose(ring[:, n % 4, k * P:(k + 1) * P],
                                            raw_a[w][:, m * D + k * P:m * D + (k + 1) * P], id32[:, :])
                    last.then_inc(wt_done, 1)
                if w == 0:
                    pe.wait_ge(aw_loaded[3], 32)
                    for g in range(KD):
                        last = pe.transpose(ug[:, 0, g * NL:(g + 1) * NL], latr[0:NL, g * P:(g + 1) * P],
                                            id32[0:NL, 0:NL])
                    last.then_inc(lat_done, 1)

            def s1(c, t, bank):
                wait(pe, xn1_ready, c, TT, t + 1)
                for k in range(KD):
                    last = pe.transpose(ring[:, bank, k * P:(k + 1) * P], xn[:, t % 2, k * P:(k + 1) * P], id32[:, :])
                last.then_inc(s1_done, 1)

            for t in range(TT):
                pe.wait_ge(wt_lo, 9 + t)
                s1(0, t, t)

            def ternary(w):
                for q in range(8):
                    n = 8 * w + q
                    pe.wait_ge(tern_ready, n + 1)
                    if n >= 2:
                        pe.wait_ge(tp_evicted, n - 1)
                    elif n == 0:
                        pe.wait_ge(lat_lo, 1)
                    src = tern[n % 2]
                    for b in range(8):
                        o = ((b % 4) * 2 + b // 4) if w < 2 else b
                        last = pe.transpose(tpb[n % 2][:, o * P:(o + 1) * P], src[:, b * P:(b + 1) * P], id16[:, :])
                    last.then_inc(tp_done, 1)

            def body(i, kind, att, ffn, nxt):
                plan = plans[kind]
                j = i - 1

                def bank_of(what, c, n):
                    bank, (pk, pc, pn) = plan[(what, c, n)]
                    s, per = FREED[pk]
                    wait(pe, s, i + pc, per, pn + 1)
                    return bank

                def project(w, bank, m, stop):
                    n = 0
                    for k in range(KD):
                        for a, b in ((0, 0), (0, 1), (1, 0)):
                            n += 1
                            last = pe.matmul(ring[:, bank, :], wT[w][a][:, k, m * P:(m + 1) * P], xT[b][:, k, :],
                                             start=(n == 1), stop=(stop and n == 3 * KD), skip_group_check=not stop)
                    return last

                def q(m):
                    bank = bank_of("Q", 0, m)
                    if m == 0:
                        wait(pe, x_lo, i, TT, TT)
                    project(0, bank, m, True).then_inc(q_done, 1)

                def t2(t):
                    bank = bank_of("T2", -1, t)
                    wait(pe, xn2_ready, j, TT, t + 1)
                    for k in range(KD):
                        last = pe.transpose(ring[:, bank, k * P:(k + 1) * P], xn[:, t % 2, k * P:(k + 1) * P], id32[:, :])
                    last.then_inc(t2_done, 1)

                def logits(t):
                    for b in range(2):
                        bank = bank_of("L", 0, 2 * t + b)
                        if t == 0 and b == 0:
                            wait(pe, q_lo, i, KD, KD)
                            if kind == "first":
                                pe.wait_ge(lat_lo, 1)
                        for g in (2 * b, 2 * b + 1):
                            for n, (a, c) in enumerate(((0, 0), (0, 1), (1, 0))):
                                last = pe.matmul(ring[:, bank, (g % 2) * 256:(g % 2) * 256 + 256],
                                                 qaT[a][:, g, t * P:(t + 1) * P], latL[c][:, g, :],
                                                 start=(n == 0), stop=(n == 2))
                        last.then_inc(l_done, 1)

                def pt(t):
                    wait(pe, p_ready, i, TT, t + 1)
                    for b in range(2):
                        bank = bank_of("PT", 0, 2 * t + b)
                        for k in range(4):
                            h = 8 * b + 2 * k
                            last = pe.transpose(ring[:, bank, k * P:(k + 1) * P], Pb[:, h * NL:(h + 2) * NL], id32[:, :])
                        last.then_inc(pt_done, 1)

                def vw(m):
                    bank = bank_of("VW", 0, m)
                    project(1, bank, m, False)
                    if m == 0:
                        wait(pe, pt_lo, i, 8, 8)
                        if kind == "first":
                            pe.wait_ge(lat_lo, 2)
                    for n, (a, c) in enumerate(((0, 0), (0, 1), (1, 0))):
                        for s in range(2):
                            last = pe.matmul(ring[64 * s:64 * s + 64, bank, :], latV[a][:, 2 * m + s, :],
                                             PT[:, c, 2 * m + s, :], start=False, stop=(n == 2), skip_group_check=True)
                    last.then_inc(vw_done, 1)

                def wo(t):
                    bank = bank_of("WO", 0, t)
                    if t == 0:
                        wait(pe, a_lo, i, KD, KD)
                    n = 0
                    for k in range(KD):
                        for a, b in ((0, 0), (0, 1), (1, 0)):
                            n += 1
                            last = pe.matmul(ring[:, bank, :], qaT[a][:, k, t * P:(t + 1) * P], wT[2][b][:, k, :],
                                             start=(n == 1), stop=(n == 3 * KD))
                    last.then_inc(wo_done, 1)

                def upgate(e):
                    if e == 0:
                        wait(pe, x1_lo, j, TT, TT)
                    wait(pe, h32_ready, j, NE, e - 1)
                    for s, w in ((0, tu), (1, tg)):
                        for k in range(KD):
                            for b in range(2):
                                last = pe.matmul(ug[:, 2 * (e % 2) + s, :], w[:, k, e * P:(e + 1) * P], X1T[:, b, k, :],
                                                 start=(k == 0 and b == 0), stop=(k == KD - 1 and b == 1))
                    last.then_inc(ug_done, 1)

                def down(t):
                    bank = bank_of("DN", -1, t)
                    for e in range(NE):
                        if t == 0:
                            wait(pe, h_lo, j, NE, e + 1)
                        for a in range(2):
                            last = pe.matmul(ring[:, bank, :], hT[:, a, e, t * P:(t + 1) * P], td[:, e, :],
                                             start=(e == 0 and a == 0), stop=(e == NE - 1 and a == 1))
                    last.then_inc(dn_done, 1)

                if att:
                    for m in range(KD):
                        q(m)
                if ffn:
                    for t in range(TT):
                        t2(t)
                if att:
                    logits(0)
                    logits(1)
                for e in range(NE):
                    if ffn:
                        upgate(e)
                    if not att:
                        continue
                    if e == 5:
                        pt(0)
                        logits(2)
                        if kind == "first":
                            ternary(0)
                    if e == 9:
                        pt(1)
                        logits(3)
                    if e == 13:
                        pt(2)
                        if kind == "first":
                            ternary(1)
                if ffn:
                    down(0)
                if att:
                    pt(3)
                if ffn:
                    down(1)
                if att:
                    for m in range(KD):
                        vw(m)
                if ffn:
                    down(2)
                    down(3)
                if nxt:
                    for t in range(TT):
                        s1(i + 1, t, bank_of("S1", 1, t))
                if att:
                    for t in range(TT):
                        wo(t)
                if kind == "first":
                    ternary(2)

            bodies(pe, body)

        @block.scalar
        def _(act):
            def abs_sum(w):
                for q in range(8):
                    n = 8 * w + q
                    act.wait_ge(w_loaded[n], 16)
                    if n:
                        act.wait_ge(asum_done, n)
                    act.activation(junk, stages[w][q], ACT.Abs, accum_out=asum[:, n:n + 1]).then_inc(asum_done, 1)

            def evict_ternary(w):
                for q in range(8):
                    n = 8 * w + q
                    act.wait_ge(tp_done, n + 1)
                    if w < 2:
                        dst = (tu, tg)[w][:, :, 256 * q:256 * q + 256]
                        src = tpb[n % 2].rearrange("p (k e) -> p k e", k=KD)
                    else:
                        dst = td[:, 8 * (q % 2):8 * (q % 2) + 8, (q // 2) * P:(q // 2 + 1) * P]
                        src = tpb[n % 2].rearrange("p (j d) -> p j d", j=8)
                    act.activation(dst, src, ACT.Copy).then_inc(tp_evicted, 1)

            act.wait_ge(scales, 1)
            for w in range(3):
                for m in range(KD):
                    n = KD * w + m
                    act.wait_ge(wt_done, n + 1)
                    act.activation(wT[w][0][:, :, m * P:(m + 1) * P],
                                   ring[:, n % 4, :].rearrange("p (k b) -> p k b", k=KD), ACT.Copy,
                                   scale=up[:, (0, 1, 3)[w]:(0, 1, 3)[w] + 1]).then_inc(wt_hi, 1)
                if w == 0:
                    act.wait_ge(lat_done, 1)
                    act.wait_ge(zeroed, 1)
                    for hh in range(4):
                        rows = slice(HD * hh, HD * hh + HD)
                        last = act.activation(latL[0][rows, :, hh * NL:(hh + 1) * NL],
                                              ug[rows, 0, 0:KD * NL].rearrange("p (g l) -> p g l", g=KD), ACT.Copy,
                                              scale=up[rows, 2:3])
                    last.then_inc(lat_hi, 1)
                    for hh in range(2):
                        rows = slice(NL * hh, NL * hh + NL)
                        last = act.activation(latV[0][rows, :, hh * HD:(hh + 1) * HD],
                                              latr[rows, :].rearrange("p (j h d) -> p j h d", h=2, d=HD)[:, :, hh, :],
                                              ACT.Copy, scale=up[rows, 1:2])
                    last.then_inc(lat_hi, 1)

            def s1_hi(c, t, bank):
                wait(act, s1_done, c, TT, t + 1)
                wait(act, vw_done, c, KD, 0)
                act.activation(xT[0][:, :, t * P:(t + 1) * P], ring[:, bank, :].rearrange("p (k b) -> p k b", k=KD),
                               ACT.Copy).then_inc(x_hi, 1)

            for t in range(TT):
                s1_hi(0, t, t)

            def body(i, kind, att, ffn, nxt):
                plan = plans[kind]
                j = i - 1

                def q(m):
                    wait(act, q_done, i, KD, m + 1)
                    if m < 2:
                        wait(act, a_lo, i - 1, KD, m + 3)
                    else:
                        wait(act, q_lo, i, KD, m - 1)
                    act.activation(p32[:, m % 2, :], ring[:, plan[("Q", 0, m)][0], :], ACT.Identity,
                                   scale=PROJ, bias=bqs[:, m:m + 1]).then_inc(q32_ready, 1)
                    wait(act, q32_ready, i, KD, m + 1)
                    wait(act, wo_done, i, TT, 0)
                    act.activation(qaT[0][:, m, :], p32[:, m % 2, :], ACT.Copy).then_inc(q_hi, 1)

                def t2(t):
                    wait(act, t2_done, j, TT, t + 1)
                    wait(act, ug_done, j, NE, 0)
                    act.activation(X1T[:, 0, :, t * P:(t + 1) * P],
                                   ring[:, plan[("T2", -1, t)][0], :].rearrange("p (k b) -> p k b", k=KD),
                                   ACT.Copy).then_inc(x1_hi, 1)

                def logits(t):
                    for b in range(2):
                        wait(act, l_done, i, 8, 2 * t + b + 1)
                        if b == 0:
                            wait(act, p_ready, i, TT, t - 1)
                            if kind == "first":
                                act.wait_ge(zeroed, 1)
                        act.activation(Lb[:, t % 2, 8 * b:8 * b + 8, 0:NL],
                                       ring[:, plan[("L", 0, 2 * t + b)][0], :].rearrange("p (h l) -> p h l", h=8),
                                       ACT.Copy, scale=clo[:, 0:1]).then_inc(l_ready, 1)

                def exp4(t):
                    wait(act, d4_ready, i, TT, t + 1)
                    act.activation(d4[:, t % 2, :, :], d4[:, t % 2, :, :], ACT.Exp).then_inc(e4_ready, 1)

                def exps(t):
                    wait(act, shifted, i, TT, t + 1)
                    act.activation(Lb[:, t % 2, :, 0:NL], Lb[:, t % 2, :, 0:NL], ACT.Exp).then_inc(e_ready, 1)

                def pt(t):
                    for b in range(2):
                        wait(act, pt_done, i, 8, 2 * t + b + 1)
                        wait(act, vw_done, i, KD, 0)
                        act.activation(PT[:, 0, 4 * b:4 * b + 4, t * P:(t + 1) * P],
                                       ring[:, plan[("PT", 0, 2 * t + b)][0], :].rearrange("p (k n) -> p k n", k=4),
                                       ACT.Copy, scale=PS).then_inc(pt_hi, 1)

                def vw(m):
                    wait(act, vw_done, i, KD, m + 1)
                    if m < 2:
                        wait(act, q_lo, i, KD, m + 3)
                    else:
                        wait(act, a_lo, i, KD, m - 1)
                    act.activation(p32[:, m % 2, :], ring[:, plan[("VW", 0, m)][0], :], ACT.Identity,
                                   scale=PROJ, bias=bvs[:, m:m + 1]).then_inc(a32_ready, 1)
                    wait(act, a32_ready, i, KD, m + 1)
                    wait(act, l_done, i, 8, 8)
                    act.activation(qaT[0][:, m, :], p32[:, m % 2, :], ACT.Copy).then_inc(a_hi, 1)

                def tanh(e):
                    wait(act, ug_done, j, NE, e + 1)
                    wait(act, h32_ready, j, NE, e - 1)
                    act.activation(ugt[:, e % 2, :], ug[:, 2 * (e % 2), :], ACT.Tanh, scale=cu[:, 0:1]).then_inc(tanh_ready, 1)

                def hidden_hi(e):
                    wait(act, h32_ready, j, NE, e + 1)
                    if e == 0:
                        wait(act, dn_done, j, TT, 0)
                    act.activation(hT[:, 0, e, :], ugt[:, 2 + e % 2, :], ACT.Copy).then_inc(h_hi, 1)

                if att:
                    for m in range(KD):
                        q(m)
                if ffn:
                    for t in range(TT):
                        t2(t)
                if att:
                    logits(0)
                    logits(1)
                for e in range(NE):
                    if ffn:
                        tanh(e)
                        if e:
                            hidden_hi(e - 1)
                    if not att:
                        continue
                    if e in (2, 4, 8, 12):
                        exp4((2, 4, 8, 12).index(e))
                    if e in (3, 6, 10, 14):
                        exps((3, 6, 10, 14).index(e))
                        if kind == "first" and e in (6, 14):
                            abs_sum((6, 14).index(e))
                            evict_ternary((6, 14).index(e))
                    if e == 5:
                        pt(0)
                        logits(2)
                    if e == 9:
                        pt(1)
                        logits(3)
                    if e == 13:
                        pt(2)
                if ffn:
                    hidden_hi(NE - 1)
                if att:
                    pt(3)
                    for m in range(KD):
                        vw(m)
                if nxt:
                    for t in range(TT):
                        s1_hi(i + 1, t, plan[("S1", 1, t)][0])
                if kind == "first":
                    abs_sum(2)
                    evict_ternary(2)

            bodies(act, body)

        @block.gpsimd
        def _(pool):
            pool.memset(id32[:, :], 0.0).then_inc(id_zeroed, 1)
            pool.memset(nh[:, :], -0.5).then_inc(consts, 1)
            pool.wait_ge(id_zeroed, 1)
            pool.affine_select(out=id32[:, :], in_=id32[:, :], compare_op=ALU.not_equal, fill=1.0, base=0,
                               pattern=[[-1, P]], channel_multiplier=1).then_inc(idents, 1)
            pool.wait_ge(mg_ready, 1)
            pool.partition_all_reduce(ma[:, :], mg[:, :], P, RMAX).then_inc(ma_ready, 1)

            def rstd(dst, src, width, var_ready, c, per, n, done):
                wait(pool, var_ready, c, per, n)
                pool.tensor_tensor(dst, src, nh[:, 0:width], ALU.pow).then_inc(done, 1)

            pool.wait_ge(consts, 1)
            rstd(rs1[:, :], va1[:, :], TT, ln1_var, 0, 1, 1, ln1_rstd)

            def all_sum(w):
                pool.wait_ge(tot_ready, w + 1)
                pool.partition_all_reduce(tota[:, w:w + 1], tot[:, w:w + 1], P, RADD).then_inc(tota_ready, 1)

            def body(i, kind, att, ffn, nxt):
                j = i - 1

                def low_q(m):
                    wait(pool, q_hi, i, KD, m + 1)
                    pool.tensor_tensor(qaT[1][:, m, :], p32[:, m % 2, :], qaT[0][:, m, :], ALU.subtract).then_inc(q_lo, 1)

                def low_a(m):
                    wait(pool, a_hi, i, KD, m + 1)
                    pool.tensor_tensor(qaT[1][:, m, :], p32[:, m % 2, :], qaT[0][:, m, :], ALU.subtract).then_inc(a_lo, 1)

                def shift(t):
                    wait(pool, replaced, i, TT, t + 1)
                    buf = Lb[:, t % 2, :, 0:NL]
                    pool.tensor_tensor(buf, buf, v8[:, t % 2, :, 0:1].broadcast_to([P, H, NL]), ALU.subtract).then_inc(shifted, 1)

                def normalise(t):
                    wait(pool, recip_ready, i, TT, t + 1)
                    wait(pool, p_raw, i, TT, t + 1)
                    wait(pool, pt_done, i, 8, 2 * t)
                    pool.tensor_tensor(Pb.rearrange("p (h l) -> p h l", h=H), Lb[:, t % 2, :, 0:NL], r4[:, t % 2, :].rearrange("p (h a) -> p h a", a=1).broadcast_to([P, H, NL]),
                                       ALU.mult).then_inc(p_ready, 1)

                def hidden_lo(e):
                    wait(pool, h_hi, j, NE, e + 1)
                    pool.tensor_tensor(hT[:, 1, e, :], ugt[:, 2 + e % 2, :], hT[:, 0, e, :], ALU.subtract).then_inc(h_lo, 1)

                def rstd_y(t):
                    rstd(rsy[:, t % 2:t % 2 + 1], vay[:, t % 2:t % 2 + 1], 1, y_var, i, TT, t + 1, y_rstd)

                def rstd_x(t):
                    rstd(rsx[:, t % 2:t % 2 + 1], vax[:, t % 2:t % 2 + 1], 1, ln2_var, i, TT, t + 1, ln2_rstd)

                def rstd_f(t):
                    rstd(rsf[:, t % 2:t % 2 + 1], vaf[:, t % 2:t % 2 + 1], 1, f_var, j, TT, t + 1, f_rstd)

                if att:
                    for m in range(KD):
                        low_q(m)
                for e in range(NE):
                    if ffn:
                        hidden_lo(e)
                    if not att:
                        continue
                    if e in (1, 4, 8, 12):
                        shift((1, 4, 8, 12).index(e))
                        if kind == "first" and e in (4, 12):
                            pass
                    if e in (2, 6, 10, 14):
                        normalise((2, 6, 10, 14).index(e))
                    if kind == "first" and e in (6, 14):
                        all_sum((6, 14).index(e))
                if ffn:
                    rstd_f(0)
                    rstd_f(1)
                if nxt:
                    rstd(rs1[:, :], va1[:, :], TT, ln1_var, i + 1, 1, 1, ln1_rstd)
                if att:
                    for m in range(KD):
                        low_a(m)
                if ffn:
                    rstd_f(2)
                    rstd_f(3)
                if att:
                    rstd_y(0)
                    rstd_y(1)
                    rstd_x(0)
                    rstd_y(2)
                    rstd_x(1)
                    rstd_y(3)
                    rstd_x(2)
                    rstd_x(3)
                if kind == "first":
                    all_sum(2)

            bodies(pool, body)

        @block.vector
        def _(dve):
            for s in range(2):
                dve.memset(latV[s][:, :, :], 0.0)
                last = dve.memset(latL[s][:, :, :], 0.0)
            dve.memset(v8[:, :, :, :], PAD)
            dve.memset(Lr[:, :, :], PAD)
            dve.memset(Lb[:, :, :, :], PAD).then_inc(zeroed, 1)
            for n, (src, s, v) in enumerate(((raw_a[0], 0, 16), (bqc[:, :], 4, 16), (raw_a[1], 1, 16), (bvc[:, :], 5, 16),
                                             (latr, 3, 32), (raw_a[2], 2, 16))):
                dve.wait_ge(aw_loaded[s], v)
                dve.tensor_reduce(mx[:, n:n + 1], src, AX.X, ALU.max, apply_absolute_value=True).then_inc(mx_ready, 1)
            dve.wait_ge(mx_ready, 6)
            dve.tensor_tensor(mg[:, 0:1], mx[:, 0:1], mx[:, 1:2], ALU.max).then_inc(sc_step, 1)
            dve.tensor_tensor(mg[:, 1:2], mx[:, 2:3], mx[:, 3:4], ALU.max).then_inc(sc_step, 1)
            dve.tensor_copy(mg[:, 2:4], mx[:, 4:6]).then_inc(sc_step, 1)
            dve.wait_ge(sc_step, 3)
            dve.tensor_tensor(mg[:, 1:2], mg[:, 1:2], mx[:, 4:5], ALU.max).then_inc(mg_ready, 1)
            dve.wait_ge(idents, 1)
            dve.tensor_copy(id16[:, :], id32[:, :]).then_inc(idents, 1)
            dve.wait_ge(ma_ready, 1)
            dve.tensor_scalar(sc[:, :], ma[:, :], TINY, None, ALU.max).then_inc(sc_step, 1)
            dve.wait_ge(sc_step, 4)
            dve.tensor_scalar(sc[:, :].bitcast(U32), sc[:, :].bitcast(U32), 0x7F800000, None, ALU.bitwise_and).then_inc(sc_step, 1)
            dve.wait_ge(sc_step, 5)
            dve.reciprocal(inv[:, :], sc[:, :]).then_inc(sc_step, 1)
            dve.tensor_tensor(clo[:, 0:1], sc[:, 0:1], sc[:, 2:3], ALU.mult).then_inc(sc_step, 1)
            dve.tensor_tensor(clo[:, 1:2], sc[:, 1:2], sc[:, 3:4], ALU.mult).then_inc(sc_step, 1)
            dve.wait_ge(sc_step, 8)
            dve.tensor_scalar(up[:, :], inv[:, :], WS, None, ALU.mult)
            dve.tensor_scalar(upb[:, :], inv[:, 0:2], AS, None, ALU.mult).then_inc(sc_step, 1)
            dve.tensor_scalar(clo[:, 0:1], clo[:, 0:1], float(HD) ** -0.5 / (AS * WS), None, ALU.mult)
            dve.tensor_scalar(clo[:, 1:2], clo[:, 1:2], 1.0 / (AS * WS), None, ALU.mult)
            dve.wait_ge(sc_step, 9)
            dve.tensor_scalar(bqs[:, :], bqc[:, :], upb[:, 0:1], None, ALU.mult)
            dve.tensor_scalar(bvs[:, :], bvc[:, :], upb[:, 1:2], None, ALU.mult).then_inc(scales, 1)

            def ln1_stat(c):
                wait(dve, x_in_loaded, c, 16, 16)
                for t in range(TT):
                    last = dve.bn_stats(st1[:, t, :], x_in[:, t, :])
                last.then_inc(ln1_stats, 1)
                wait(dve, ln1_stats, c, 1, 1)
                dve.sem_inc(own_wait, 1)
                for t in range(TT):
                    last = dve.bn_aggr(mv1[:, t, :], st1[:, t, :])
                last.then_inc(ln1_mean, 1)
                wait(dve, ln1_mean, c, 1, 1)
                dve.tensor_scalar(va1[:, :], mv1[:, :, 1], XS ** -2, EPS * XS ** -2, ALU.mult, ALU.add).then_inc(ln1_var, 1)

            def ln1_apply(c, t):
                wait(dve, ln1_rstd, c, 1, 1)
                if t < 2:
                    wait(dve, t2_done, c - 2, TT, t + 3)
                else:
                    wait(dve, s1_done, c, TT, t - 1)
                dve.tensor_scalar(xn[:, t % 2, :], x_in[:, t, :], mv1[:, t, 0:1], rs1[:, t:t + 1],
                                  ALU.subtract, ALU.mult).then_inc(xn1_ready, 1)

            def s1_lo(c, t, bank):
                wait(dve, x_hi, c, TT, t + 1)
                dve.tensor_tensor(xT[1][:, :, t * P:(t + 1) * P], ring[:, bank, :].rearrange("p (k b) -> p k b", k=KD),
                                  xT[0][:, :, t * P:(t + 1) * P], ALU.subtract).then_inc(x_lo, 1)

            ln1_stat(0)
            for w in range(3):
                for m in range(KD):
                    n = KD * w + m
                    dve.wait_ge(wt_hi, n + 1)
                    dve.scalar_tensor_tensor(out=wT[w][1][:, :, m * P:(m + 1) * P],
                                             in0=ring[:, n % 4, :].rearrange("p (k b) -> p k b", k=KD),
                                             scalar=up[:, (0, 1, 3)[w]:(0, 1, 3)[w] + 1],
                                             in1=wT[w][0][:, :, m * P:(m + 1) * P],
                                             op0=ALU.mult, op1=ALU.subtract).then_inc(wt_lo, 1)
                if w == 0:
                    dve.wait_ge(lat_hi, 2)
                    for hh in range(4):
                        rows = slice(HD * hh, HD * hh + HD)
                        last = dve.scalar_tensor_tensor(out=latL[1][rows, :, hh * NL:(hh + 1) * NL],
                                                        in0=ug[rows, 0, 0:KD * NL].rearrange("p (g l) -> p g l", g=KD),
                                                        scalar=up[rows, 2:3], in1=latL[0][rows, :, hh * NL:(hh + 1) * NL],
                                                        op0=ALU.mult, op1=ALU.subtract)
                    last.then_inc(lat_lo, 1)
                    for hh in range(2):
                        rows = slice(NL * hh, NL * hh + NL)
                        last = dve.scalar_tensor_tensor(out=latV[1][rows, :, hh * HD:(hh + 1) * HD],
                                                        in0=latr[rows, :].rearrange("p (j h d) -> p j h d", h=2, d=HD)[:, :, hh, :],
                                                        scalar=up[rows, 1:2], in1=latV[0][rows, :, hh * HD:(hh + 1) * HD],
                                                        op0=ALU.mult, op1=ALU.subtract)
                    last.then_inc(lat_lo, 1)
            ln1_apply(0, 0)
            ln1_apply(0, 1)
            for t in range(TT):
                s1_lo(0, t, t)
                if t < 2:
                    ln1_apply(0, t + 2)

            def ternarise(w):
                dve.wait_ge(asum_done, 8 * w + 8)
                dve.reduce_sum(tot[:, w:w + 1], asum[:, 8 * w:8 * w + 8], AX.X).then_inc(tot_ready, 1)
                dve.wait_ge(tota_ready, w + 1)
                dve.tensor_scalar(sw[:, w:w + 1], tota[:, w:w + 1], 1.0 / (E * D), QEPS, ALU.mult, ALU.add).then_inc(tern_step, 1)
                dve.wait_ge(tern_step, w + 1)
                dve.tensor_scalar(hw[:, w:w + 1], sw[:, w:w + 1], 0.5, None, ALU.mult)
                dve.tensor_scalar(nhw[:, w:w + 1], sw[:, w:w + 1], -0.5, None, ALU.mult).then_inc(tern_scale, 1)
                dve.wait_ge(tern_scale, w + 1)
                for q in range(8):
                    n = 8 * w + q
                    if n:
                        dve.wait_ge(tern_ready, n)
                    else:
                        dve.wait_ge(lat_lo, 2)
                    dve.tensor_scalar(belowb, stages[w][q], nhw[:, w:w + 1], None, ALU.is_lt).then_inc(below, 1)
                    dve.wait_ge(below, n + 1)
                    if n >= 2:
                        dve.wait_ge(tp_done, n - 1)
                    dve.scalar_tensor_tensor(out=tern[n % 2], in0=stages[w][q], scalar=hw[:, w:w + 1], in1=belowb,
                                             op0=ALU.is_gt, op1=ALU.subtract).then_inc(tern_ready, 1)
                if w == 2:
                    dve.tensor_scalar(cu[:, :], sw[:, 0:1], 0.5 / XS, None, ALU.mult)
                    dve.tensor_tensor(cf[:, 0:1], sw[:, 0:1], sw[:, 1:2], ALU.mult).then_inc(tern_step, 1)
                    dve.wait_ge(tern_step, 4)
                    dve.scalar_tensor_tensor(out=cf[:, 1:2], in0=cf[:, 0:1], scalar=0.5 / (XS * XS * HS), in1=sw[:, 2:3],
                                             op0=ALU.mult, op1=ALU.mult).then_inc(tern_step, 1)
                    dve.wait_ge(tern_step, 5)

            def body(i, kind, att, ffn, nxt):
                plan = plans[kind]
                j = i - 1

                def t2_lo(t):
                    wait(dve, x1_hi, j, TT, t + 1)
                    dve.tensor_tensor(X1T[:, 1, :, t * P:(t + 1) * P],
                                      ring[:, plan[("T2", -1, t)][0], :].rearrange("p (k b) -> p k b", k=KD),
                                      X1T[:, 0, :, t * P:(t + 1) * P], ALU.subtract).then_inc(x1_lo, 1)

                def hidden(e):
                    wait(dve, tanh_ready, j, NE, e + 1)
                    dve.scalar_tensor_tensor(out=ugt[:, e % 2, :], in0=ugt[:, e % 2, :], scalar=1.0,
                                             in1=ug[:, 2 * (e % 2), :], op0=ALU.add, op1=ALU.mult).then_inc(t1_ready, 1)
                    wait(dve, t1_ready, j, NE, e + 1)
                    wait(dve, h_lo, j, NE, e - 1)
                    dve.scalar_tensor_tensor(out=ugt[:, 2 + e % 2, :], in0=ugt[:, e % 2, :], scalar=HS,
                                             in1=ug[:, 2 * (e % 2) + 1, :], op0=ALU.mult, op1=ALU.mult).then_inc(h32_ready, 1)

                def maxes(t, b):
                    wait(dve, l_ready, i, 8, 2 * t + b + 1)
                    if b == 0:
                        wait(dve, shifted, i, TT, t - 1)
                    dve.sem_inc(own_wait, 1)
                    for h in range(8 * b, 8 * b + 8):
                        last = dve.max(v8[:, t % 2, h, :], Lb[:, t % 2, h, 0:NL])
                    if b:
                        last.then_inc(top8, 1)

                def slots(t):
                    wait(dve, top8, i, TT, t + 1)
                    dve.memset(v8[:, t % 2, :, TOPK:8], PAD).then_inc(v8_ready, 1)
                    wait(dve, recip_ready, i, TT, t - 1)
                    dve.tensor_tensor(d4[:, t % 2, :, :], v8[:, t % 2, :, 0:TOPK],
                                      v8[:, t % 2, :, 0:1].broadcast_to([P, H, TOPK]), ALU.subtract).then_inc(d4_ready, 1)

                def replace(t, b):
                    wait(dve, v8_ready, i, TT, t + 1)
                    wait(dve, p_raw, i, TT, t)
                    dve.sem_inc(own_wait, 1)
                    for h in range(8 * b, 8 * b + 8):
                        last = dve.match_replace(Lr[:, h, :], v8[:, t % 2, h, :], Lb[:, t % 2, h, :], HIT)
                    if b:
                        last.then_inc(replaced, 1)

                def sums(t):
                    wait(dve, e4_ready, i, TT, t + 1)
                    dve.tensor_reduce(s4[:, t % 2, :], d4[:, t % 2, :, :], AX.X, ALU.add).then_inc(sum_ready, 1)
                    wait(dve, sum_ready, i, TT, t + 1)
                    wait(dve, p_ready, i, TT, t - 1)
                    dve.reciprocal(r4[:, t % 2, :], s4[:, t % 2, :]).then_inc(recip_ready, 1)

                def select(t):
                    wait(dve, e_ready, i, TT, t + 1)
                    buf = Lb[:, t % 2, :, 0:NL]
                    dve.scalar_tensor_tensor(out=buf, in0=Lr[:, :, 0:NL], scalar=HIT, in1=buf,
                                             op0=ALU.is_equal, op1=ALU.mult).then_inc(p_raw, 1)

                def pt_low(t):
                    for b in range(2):
                        wait(dve, pt_hi, i, 8, 2 * t + b + 1)
                        dve.scalar_tensor_tensor(out=PT[:, 1, 4 * b:4 * b + 4, t * P:(t + 1) * P],
                                                 in0=ring[:, plan[("PT", 0, 2 * t + b)][0], :].rearrange("p (k n) -> p k n", k=4),
                                                 scalar=PS, in1=PT[:, 0, 4 * b:4 * b + 4, t * P:(t + 1) * P],
                                                 op0=ALU.mult, op1=ALU.subtract).then_inc(pt_lo, 1)

                def f_a(t):
                    s = t % 2
                    bank = plan[("DN", -1, t)][0]
                    wait(dve, dn_done, j, TT, t + 1)
                    dve.bn_stats(stf[:, s, :], ring[:, bank, :]).then_inc(f_stats, 1)
                    wait(dve, f_stats, j, TT, t + 1)
                    dve.sem_inc(own_wait, 1)
                    dve.bn_aggr(mvf[:, s, :], stf[:, s, :]).then_inc(f_mean, 1)
                    wait(dve, f_mean, j, TT, t + 1)
                    dve.tensor_scalar(vaf[:, s:s + 1], mvf[:, s, 1:2], cf[:, 1:2], cf[:, 1:2], ALU.mult, ALU.mult).then_inc(f_varc, 1)
                    wait(dve, f_varc, j, TT, t + 1)
                    dve.tensor_scalar(vaf[:, s:s + 1], vaf[:, s:s + 1], EPS, None, ALU.add).then_inc(f_var, 1)

                def f_b(t):
                    s = t % 2
                    bank = plan[("DN", -1, t)][0]
                    wait(dve, f_rstd, j, TT, t + 1)
                    dve.tensor_tensor(rcf[:, s:s + 1], rsf[:, s:s + 1], cf[:, 1:2], ALU.mult).then_inc(f_scale, 1)
                    wait(dve, f_scale, j, TT, t + 1)
                    if t >= 2:
                        wait(dve, out_stored[s], j, 32, 16)
                    dve.tensor_scalar(row[:, s, :], ring[:, bank, :], mvf[:, s, 0:1], rcf[:, s:s + 1],
                                      ALU.subtract, ALU.mult).then_inc(f_norm, 1)
                    wait(dve, f_norm, j, TT, t + 1)
                    dve.tensor_tensor(row[:, s, :], row[:, s, :], x1[:, t, :], ALU.add).then_inc(out_ready, 1)

                def y_a(t):
                    s = t % 2
                    wait(dve, wo_done, i, TT, t + 1)
                    if t < 2:
                        wait(dve, out_stored[s], i, 32, 0)
                        if kind == "first":
                            dve.wait_ge(tp_done, 16)
                            dve.wait_ge(aw_loaded[6], 16)
                    dve.scalar_tensor_tensor(out=row[:, s, :], in0=ring[:, plan[("WO", 0, t)][0], :], scalar=clo[:, 1:2],
                                             in1=bo_b[:, :], op0=ALU.mult, op1=ALU.add).then_inc(y_ready, 1)
                    wait(dve, y_ready, i, TT, t + 1)
                    dve.bn_stats(sty[:, s, :], row[:, s, :]).then_inc(y_stats, 1)
                    wait(dve, y_stats, i, TT, t + 1)
                    dve.sem_inc(own_wait, 1)
                    dve.bn_aggr(mvy[:, s, :], sty[:, s, :]).then_inc(y_mean, 1)
                    wait(dve, y_mean, i, TT, t + 1)
                    dve.tensor_scalar(vay[:, s:s + 1], mvy[:, s, 1:2], EPS, None, ALU.add).then_inc(y_var, 1)

                def y_b(t):
                    s = t % 2
                    wait(dve, y_rstd, i, TT, t + 1)
                    dve.tensor_scalar(row[:, s, :], row[:, s, :], mvy[:, s, 0:1], rsy[:, s:s + 1],
                                      ALU.subtract, ALU.mult).then_inc(z_ready, 1)
                    wait(dve, z_ready, i, TT, t + 1)
                    wait(dve, x_res_loaded[t], i, 16, 16)
                    dve.tensor_tensor(x1[:, t, :], row[:, s, :], x1[:, t, :], ALU.add).then_inc(x1_ready, 1)
                    wait(dve, x1_ready, i, TT, t + 1)
                    dve.bn_stats(stx[:, s, :], x1[:, t, :]).then_inc(ln2_stats, 1)
                    wait(dve, ln2_stats, i, TT, t + 1)
                    dve.sem_inc(own_wait, 1)
                    dve.bn_aggr(mvx[:, s, :], stx[:, s, :]).then_inc(ln2_mean, 1)
                    wait(dve, ln2_mean, i, TT, t + 1)
                    dve.tensor_scalar(vax[:, s:s + 1], mvx[:, s, 1:2], XS ** -2, EPS * XS ** -2, ALU.mult, ALU.add).then_inc(ln2_var, 1)

                def y_c(t):
                    s = t % 2
                    wait(dve, ln2_rstd, i, TT, t + 1)
                    if t >= 2:
                        wait(dve, t2_done, i, TT, t - 1)
                    elif nxt:
                        wait(dve, s1_done, i + 1, TT, t + 3)
                    else:
                        wait(dve, t2_done, i - 1, TT, t + 3)
                    dve.tensor_scalar(xn[:, s, :], x1[:, t, :], mvx[:, s, 0:1], rsx[:, s:s + 1],
                                      ALU.subtract, ALU.mult).then_inc(xn2_ready, 1)

                if ffn:
                    for t in range(TT):
                        t2_lo(t)
                AFTER = {0: [(maxes, 0, 0)], 1: [(maxes, 0, 1), (slots, 0), (replace, 0, 0)],
                         2: [(replace, 0, 1), (maxes, 1, 0)], 3: [(sums, 0), (select, 0), (maxes, 1, 1), (slots, 1)],
                         4: [(replace, 1, 0)], 5: [(replace, 1, 1), (pt_low, 0)],
                         6: [(sums, 1), (select, 1), (maxes, 2, 0)], 7: [(maxes, 2, 1), (slots, 2)],
                         8: [(replace, 2, 0)], 9: [(replace, 2, 1), (pt_low, 1)],
                         10: [(sums, 2), (select, 2)], 11: [(maxes, 3, 0), (maxes, 3, 1), (slots, 3)],
                         12: [(replace, 3, 0)], 13: [(replace, 3, 1), (pt_low, 2)],
                         14: [(sums, 3), (select, 3)], 15: []}
                for e in range(NE):
                    if ffn:
                        hidden(e)
                    if att:
                        for f, *a in AFTER[e]:
                            f(*a)
                        if kind == "first" and e in (6, 14):
                            ternarise((6, 14).index(e))
                if ffn:
                    f_a(0)
                if att:
                    pt_low(3)
                if ffn:
                    f_b(0)
                    f_a(1)
                if nxt:
                    ln1_stat(i + 1)
                if ffn:
                    f_b(1)
                if nxt:
                    ln1_apply(i + 1, 0)
                    ln1_apply(i + 1, 1)
                if ffn:
                    f_a(2)
                    f_b(2)
                    f_a(3)
                    f_b(3)
                if nxt:
                    for t in range(TT):
                        s1_lo(i + 1, t, plan[("S1", 1, t)][0])
                        if t < 2:
                            ln1_apply(i + 1, t + 2)
                if att:
                    y_a(0)
                    y_a(1)
                    y_b(0)
                    y_a(2)
                    y_b(1)
                    y_c(0)
                    y_a(3)
                    y_b(2)
                    y_c(1)
                    y_b(3)
                    if kind != "first":
                        y_c(2)
                        y_c(3)
                if kind == "first":
                    ternarise(2)
                    y_c(2)
                    y_c(3)

            bodies(dve, body)


_INS = ["L0_attn_hidden_states", "L0_attn_Wq", "L0_attn_bq", "L0_attn_Wv", "L0_attn_bv", "L0_attn_Wo", "L0_attn_bo",
        "L0_attn_latent_keys", "L0_ffn_W_up", "L0_ffn_W_gate", "L0_ffn_W_down"]


def kernel(**inputs):
    import numpy as _np
    import concourse.bacc as _bacc
    from concourse import mybir as _mybir
    from concourse.bass_utils import run_bass_kernel_spmd as _run

    nc = _bacc.Bacc("TRN2", target_bir_lowering=False, num_devices=1)
    arrays, args = {}, []
    for name in _INS:
        a = _np.ascontiguousarray(inputs[name])
        arrays[f"in_{name}"] = a
        args.append(nc.dram_tensor(f"in_{name}", a.shape, _mybir.dt.from_np(a.dtype), kind="ExternalInput").ap())
    shape = inputs["L0_attn_hidden_states"].shape
    o = nc.dram_tensor("out_dram", shape, _mybir.dt.float32, kind="ExternalOutput").ap()
    build(nc, *args, o)
    r = _run(nc, [arrays], core_ids=[0])
    return r.results[0]["out_dram"]
```

```python
from contextlib import ExitStack

import concourse.bass as bass
from concourse import mybir

ALU = mybir.AluOpType
ACT = mybir.ActivationFunctionType
AX = mybir.AxisListType
F32 = mybir.dt.float32
F16 = mybir.dt.float16
U32 = mybir.dt.uint32
RMAX = bass.bass_isa.ReduceOp.max
RADD = bass.bass_isa.ReduceOp.add

P = 128
D = 512
KD = D // P
H = 16
HD = D // H
NL = 64
TOPK = 4
E = 2048
NE = E // P
TT = 4
CH = TT * P
PADS = 8 - TOPK
LW = NL + PADS
EPS = 1e-5
QEPS = 1e-8

PAD = -3.0e38
HIT = -1.0e30
XS = 2.0 ** 11
WS = 2.0 ** 13
AS = 2.0 ** 5
PROJ = AS / (XS * WS)
PS = 2.0 ** 11
HS = 2.0 ** -26
TINY = 2.0 ** -100

def pe_order(kind):
    att, ffn, nxt = kind != "tail", kind != "first", kind in ("first", "mid")
    o = []
    if kind == "first":
        o += [("S1", 0, t) for t in range(TT)] + [("WT", 0, n) for n in range(KD)]
    if att:
        o += [("Q", 0, m) for m in range(KD)]
    if ffn and att:
        o += [("T2", -1, 2), ("T2", -1, 3)]
    if att:
        o += [("L", 0, n) for n in range(4)]
        if kind == "first":
            o += [("WT", 0, n) for n in range(KD, 3 * KD)]
        for t in range(TT - 1):
            o += [("PT", 0, 2 * t), ("PT", 0, 2 * t + 1)]
            if t < 2:
                o += [("L", 0, 2 * t + 4), ("L", 0, 2 * t + 5)]
    if ffn:
        o += [("DN", -1, 0)]
    if att:
        o += [("PT", 0, 6), ("PT", 0, 7)]
    if ffn:
        o += [("DN", -1, 1)]
    if att:
        o += [("VW", 0, m) for m in range(KD)]
    if nxt:
        o += [("S1", 1, 0), ("S1", 1, 1)]
    if ffn:
        o += [("DN", -1, 2)]
    if kind == "last":
        o += [("WO", 0, t) for t in range(TT)] + [("T2", 0, 0), ("T2", 0, 1), ("DN", -1, 3), ("T2", 0, 2), ("T2", 0, 3)]
        return o
    if att:
        o += [("WO", 0, 0), ("WO", 0, 1)]
    if nxt:
        o += [("S1", 1, 2), ("S1", 1, 3)]
    if ffn:
        o += [("DN", -1, 3)]
    if att:
        o += [("WO", 0, 2), ("WO", 0, 3), ("T2", 0, 0), ("T2", 0, 1)]
    return o


def ring_plan(kind):
    if kind == "first":
        seq = pe_order(kind)
        shift = -len(seq) % 4
        return {job: ((n + shift) % 4, seq[n - 4] if n >= 4 else None) for n, job in enumerate(seq)}
    before = [(w, c - 1, n) for w, c, n in pe_order("first" if kind == "mid" else "mid" if kind == "last" else "last")[-4:]]
    seq = before + pe_order(kind)
    return {seq[n]: (n % 4, seq[n - 4]) for n in range(4, len(seq))}


def build(nc, x, Wq, bq, Wv, bv, Wo, bo, lat, Wu, Wg, Wd, out):
    NCH = x.shape[0] * x.shape[1] // CH
    with ExitStack() as ctx:
        def sb(name, shape, dt=F32):
            return ctx.enter_context(nc.sbuf_tensor(name, shape, dt))

        def sem(name):
            return ctx.enter_context(nc.semaphore(name))

        TU = sb("TU", [P, KD * E], F16)
        TG = sb("TG", [P, KD * E], F16)
        TD = sb("TD", [P, NE * D], F16)
        tu = TU[:, :].rearrange("p (k e) -> p k e", k=KD)
        tg = TG[:, :].rearrange("p (k e) -> p k e", k=KD)
        td = TD[:, :].rearrange("p (j d) -> p j d", j=NE)
        wT = [[sb(f"w{w}_{s}", [P, KD, D], F16) for s in ("hi", "lo")] for w in ("q", "v", "o")]
        latL = [sb(f"latL_{s}", [P, KD, 4 * NL], F16) for s in ("hi", "lo")]
        latV = [sb(f"latV_{s}", [P, H // 2, 2 * HD], F16) for s in ("hi", "lo")]
        bo_b = sb("bo_b", [P, D])
        id32 = sb("id32", [P, P])
        id16 = sb("id16", [P, P], F16)

        x_in = sb("x_in", [P, TT, D])
        x1 = sb("x1", [P, TT, D])
        xT = [sb(f"xT_{s}", [P, KD, CH], F16) for s in ("hi", "lo")]
        qaT = [sb(f"qaT_{s}", [P, KD, CH], F16) for s in ("hi", "lo")]
        Lb = sb("Lb", [P, 2, H, LW])
        Lr = sb("Lr", [P, H, LW])
        PT = sb("PT", [P, 2, 8, CH], F16)
        X1T = sb("X1T", [P, 2, KD, CH], F16)
        hT = sb("hT", [P, 2, NE, CH], F16)
        ugt = sb("ugt", [P, 4, CH])
        p32 = sb("p32", [P, 2, CH])
        Pb = p32[:, :, :].rearrange("p a b -> p (a b)")
        row = sb("row", [P, 2, D])
        xn = sb("xn", [P, 2, D])

        mv1 = sb("mv1", [P, TT, 2])
        st1 = sb("st1", [P, TT, 6])
        sty = sb("sty", [P, 2, 6])
        mvy = sb("mvy", [P, 2, 2])
        stx = sb("stx", [P, 2, 6])
        mvx = sb("mvx", [P, 2, 2])
        stf = sb("stf", [P, 2, 6])
        mvf = sb("mvf", [P, 2, 2])
        va1 = sb("va1", [P, TT])
        vay = sb("vay", [P, 2])
        vax = sb("vax", [P, 2])
        vaf = sb("vaf", [P, 2])
        rs1 = sb("rs1", [P, TT])
        rsy = sb("rsy", [P, 2])
        rsx = sb("rsx", [P, 2])
        rsf = sb("rsf", [P, 2])
        rcf = sb("rcf", [P, 2])
        nb1 = sb("nb1", [P, TT])
        nbx = sb("nbx", [P, 2])
        nby, nby_last = sb("nby", [P, TT]), sb("nby_last", [P, TT])
        nbf = sb("nbf", [P, 2])
        nh = sb("nh", [P, TT])
        v8 = sb("v8", [P, 2, H, 8])
        d4 = sb("d4", [P, 2, H, TOPK])
        s4 = sb("s4", [P, 2, H])
        r4 = sb("r4", [P, 2, H])
        bqc = sb("bqc", [P, KD])
        bvc = sb("bvc", [P, KD])
        bqs = sb("bqs", [P, KD])
        bvs = sb("bvs", [P, KD])
        mx = sb("mx", [P, 6])
        mg = sb("mg", [P, 4])
        ma = sb("ma", [P, 4])
        sc = sb("sc", [P, 4])
        inv = sb("inv", [P, 4])
        up = sb("upw", [P, 4])
        upb = sb("upb", [P, 2])
        clo = sb("clo", [P, 2])
        asum = sb("asum", [P, 24])
        tot = sb("tot", [P, 3])
        tota = sb("tota", [P, 3])
        sw = sb("sw", [P, 3])
        hw = sb("hw", [P, 3])
        nhw = sb("nhw", [P, 3])
        cu = sb("cu", [P, 1])
        cf = sb("cf", [P, 2])

        ug = ctx.enter_context(nc.psum_tensor("ug", [P, 4, CH], F32))
        ring = ctx.enter_context(nc.psum_tensor("ring", [P, 4, CH], F32))

        PER = {}

        def csem(name, n):
            PER[name] = n
            return sem(name)

        x_in_loaded = csem("x_in_loaded", 16)
        x_res_loaded = [sem(f"x_res_loaded{t}") for t in range(TT)]
        out_stored = [sem(f"out_stored{t}") for t in range(TT)]
        ln1_stats, ln1_mean, ln1_var, ln1_rstd, ln1_bias = (sem(f"ln1_{n}") for n in ("stats", "mean", "var", "rstd", "bias"))
        xn1_ready = sem("xn1_ready")
        s1_done, x_hi, x_lo = sem("s1_done"), sem("x_hi"), sem("x_lo")
        q_done, q32_ready, q_hi, q_lo = sem("q_done"), sem("q32_ready"), sem("q_hi"), sem("q_lo")
        l_done, l_ready = sem("l_done"), sem("l_ready")
        top8, v8_ready, d4_ready, e4_ready = sem("top8"), sem("v8_ready"), sem("d4_ready"), sem("e4_ready")
        sum_ready, recip_ready = sem("sum_ready"), sem("recip_ready")
        replaced, shifted, e_ready = sem("replaced"), sem("shifted"), sem("e_ready")
        p_raw, p_ready = sem("p_raw"), sem("p_ready")
        pt_done, pt_hi, pt_lo = sem("pt_done"), sem("pt_hi"), sem("pt_lo")
        vw_done, a32_ready, a_hi, a_lo = sem("vw_done"), sem("a32_ready"), sem("a_hi"), sem("a_lo")
        wo_done, y_ready = sem("wo_done"), sem("y_ready")
        y_stats, y_mean, y_var, y_rstd = (sem(f"y_{n}") for n in ("stats", "mean", "var", "rstd"))
        x1_ready = sem("x1_ready")
        ln2_stats, ln2_mean, ln2_var, ln2_rstd, ln2_bias = (sem(f"ln2_{n}") for n in ("stats", "mean", "var", "rstd", "bias"))
        xn2_ready = sem("xn2_ready")
        t2_done, x1_hi, x1_lo = sem("t2_done"), sem("x1_hi"), sem("x1_lo")
        ug_done, tanh_ready, t1_ready, h32_ready = sem("ug_done"), sem("tanh_ready"), sem("t1_ready"), sem("h32_ready")
        h_hi, h_lo = sem("h_hi"), sem("h_lo")
        dn_done = sem("dn_done")
        f_stats, f_mean, f_var, f_rstd, f_scale, f_bias, f_sum = (sem(f"f_{n}") for n in ("stats", "mean", "var", "rstd", "scale", "bias", "sum"))
        f_varc = sem("f_varc")
        out_ready = sem("out_ready")
        own_wait = sem("own_wait")
        aw_loaded = [sem(f"aw_loaded{n}") for n in range(7)]
        w_loaded = [sem(f"w_loaded{n}") for n in range(24)]
        zeroed, id_zeroed, consts, idents = sem("zeroed"), sem("id_zeroed"), sem("consts"), sem("idents")
        mx_ready, mg_ready, ma_ready, sc_step, scales = (sem(n) for n in ("mx_ready", "mg_ready", "ma_ready", "sc_step", "scales"))
        wt_done, wt_hi, wt_lo = sem("wt_done"), sem("wt_hi"), sem("wt_lo")
        lat_done, lat_hi, lat_lo = sem("lat_done"), sem("lat_hi"), sem("lat_lo")
        asum_done, tot_ready, tota_ready, tern_step = (sem(n) for n in ("asum_done", "tot_ready", "tota_ready", "tern_step"))
        tern_scale = sem("tern_scale")
        own_below, own_asum = sem("own_below"), sem("own_asum")
        below_ready, tern_ready, tp_done, tp_evicted = (sem(n) for n in ("below_ready", "tern_ready", "tp_done", "tp_evicted"))

        FREED = {"S1": (x_lo, TT), "Q": (q32_ready, KD), "T2": (x1_lo, TT), "L": (l_ready, 8), "PT": (pt_lo, 8),
                 "DN": (f_sum, TT), "WT": (wt_lo, 3 * KD), "VW": (a32_ready, KD), "WO": (y_ready, TT)}

        def wait(eng, s, c, per, n):
            v = c * per + max(n, 0)
            if not isinstance(v, int) or v > 0:
                eng.wait_ge(s, v)

        hT32 = hT[:, :, :, :].rearrange("p s e t -> p (s e t)").bitcast(F32)
        td32 = TD[:, :].bitcast(F32)
        x1t32 = X1T[:, :, :, :].rearrange("p s k t -> p (s k t)").bitcast(F32)
        ugt32 = ugt[:, :, :].rearrange("p a b -> p (a b)")
        tg32 = TG[:, :].bitcast(F32)
        raw_a = [TU[:, :].bitcast(F32)[:, 0:2048], tg32[:, 0:2048], tg32[:, 2048:4096]]
        latr = row[:, 0, :]
        stage_hT = [hT32[:, 1024 * q:1024 * q + 1024] for q in range(8)]
        stage_mix = ([td32[:, 1024 * q:1024 * q + 1024] for q in range(4)]
                     + [x1t32[:, 1024 * q:1024 * q + 1024] for q in range(2)]
                     + [ugt32[:, 1024 * q:1024 * q + 1024] for q in range(2)])
        stages = [stage_hT, stage_mix, stage_hT]
        slots_a = [x1[:, s, :].bitcast(F16) for s in range(TT)]
        slots_d = [ugt[:, s, :].bitcast(F16) for s in range(4)]
        tern = [(slots_a if n < 16 else slots_d)[n % 4] for n in range(24)]
        ASUM_DVE = (4, 5, 6, 7)
        BELOW_DVE = (0, 1, 5, 7, 8, 9, 11, 13, 15, 16, 17, 19, 20, 21, 22, 23)
        tpb = [ug[:, s, :].bitcast(F16) for s in range(2)]
        junk = ug[:, 2:4, :].rearrange("p a b -> p (a b)")

        xv = x.rearrange("b (c p t) d -> (b c) p t d", p=P, t=TT)
        ov = out.rearrange("b (c p t) d -> (b c) p t d", p=P, t=TT)

        def residual(is_last):
            return x_in if is_last else x1

        def slot_free(eng, n):
            if 16 <= n < 20:
                eng.wait_ge(tern_ready, 16)
            elif n >= 4:
                eng.wait_ge(tp_done, n - 3)

        def chunk(v, c):
            return v[c] if isinstance(c, int) else v[bass.ds(c, 1)].rearrange("a p t d -> (a p) t d")

        plans = {kind: ring_plan(kind) for kind in ("first", "mid", "last", "tail")}

        def bodies(eng, body):
            body(0, "first", True, False, True)
            with eng.Fori(1, NCH - 1) as i:
                body(i, "mid", True, True, True)
            body(NCH - 1, "last", True, True, False)
            body(NCH, "tail", False, True, False)

        WSCALE = (0, 2, 3)

        block = ctx.enter_context(nc.Block())

        @block.sync
        def _(sp):
            def load_ffn(w, W):
                v = W.rearrange("(q r p) d -> q p r d", p=P, r=2)
                for q in range(8):
                    sp.dma_start(stages[w][q].rearrange("p (r d) -> p r d", r=2), v[q]).then_inc(w_loaded[8 * w + q], 16)

            sp.dma_start(x_in[:, :, :], xv[0]).then_inc(x_in_loaded, 16)
            sp.dma_start(raw_a[0].rearrange("p (m d) -> p m d", m=KD), Wq.rearrange("(m p) d -> p m d", p=P)).then_inc(aw_loaded[0], 16)
            for s in range(2):
                sp.dma_start(latr[NL * s:NL * s + NL, :], lat).then_inc(aw_loaded[3], 16)
            sp.dma_start(bqc[:, :], bq.rearrange("(m p) -> p m", p=P), allow_slow_non_contiguous=True).then_inc(aw_loaded[4], 16)
            load_ffn(0, Wu)
            sp.dma_start(bvc[:, :], bv.rearrange("(m p) -> p m", p=P), allow_slow_non_contiguous=True).then_inc(aw_loaded[5], 16)
            sp.dma_start(raw_a[1].rearrange("p (m d) -> p m d", m=KD), Wv.rearrange("(m p) d -> p m d", p=P)).then_inc(aw_loaded[1], 16)
            sp.dma_start(raw_a[2].rearrange("p (m d) -> p m d", m=KD), Wo.rearrange("(m p) d -> p m d", p=P)).then_inc(aw_loaded[2], 16)
            load_ffn(1, Wg)
            sp.dma_start(bo_b[:, :], bo.rearrange("(a d) -> a d", a=1).broadcast_to([P, D])).then_inc(aw_loaded[6], 16)

            def body(i, kind, att, ffn, nxt):
                if nxt:
                    wait(sp, xn1_ready, i, TT, TT)
                    sp.dma_start(x_in[:, :, :], chunk(xv, i + 1)).then_inc(x_in_loaded, 16)
                if kind == "first":
                    v = Wd.rearrange("(a p) (b e) -> a b p e", p=P, b=2)
                    for q in range(8):
                        sp.wait_ge(tern_ready, q + 1)
                        sp.dma_start(stages[2][q], v[q // 2, q % 2]).then_inc(w_loaded[16 + q], 16)
                    sp.wait_ge(tp_done, 16)
                    for t in range(TT):
                        sp.dma_start(x1[:, t, :], xv[0, :, t, :]).then_inc(x_res_loaded[t], 16)
                if ffn:
                    for t in range(TT):
                        wait(sp, out_ready, i - 1, TT, t + 1)
                        sp.dma_start(chunk(ov, i - 1)[:, t, :], residual(kind == "tail")[:, t, :]).then_inc(out_stored[t], 16)
                        if nxt:
                            wait(sp, out_stored[t], i, 16, 0)
                            sp.dma_start(x1[:, t, :], chunk(xv, i)[:, t, :]).then_inc(x_res_loaded[t], 16)

            bodies(sp, body)
            for t in range(TT):
                sp.wait_ge(out_stored[t], 16 * NCH)

        @block.tensor
        def _(pe):
            def body(i, kind, att, ffn, nxt):
                plan = plans[kind]
                j = i - 1

                def bank_of(what, c, n):
                    bank, before = plan[(what, c, n)]
                    if before:
                        pk, pc, pn = before
                        s, per = FREED[pk]
                        wait(pe, s, i + pc, per, pn + 1)
                    return bank

                def transposed_rows(bank, t):
                    for k in range(KD):
                        last = pe.transpose(ring[:, bank, k * P:(k + 1) * P], xn[:, t % 2, k * P:(k + 1) * P], id32[:, :])
                    return last

                def s1(c, t):
                    bank = bank_of("S1", c, t)
                    wait(pe, xn1_ready, i + c, TT, t + 1)
                    transposed_rows(bank, t).then_inc(s1_done, 1)

                def t2(c, t):
                    bank = bank_of("T2", c, t)
                    wait(pe, xn2_ready, i + c, TT, t + 1)
                    transposed_rows(bank, t).then_inc(t2_done, 1)

                def weights(w):
                    pe.wait_ge(aw_loaded[w], 16)
                    for m in range(KD):
                        bank = bank_of("WT", 0, KD * w + m)
                        for k in range(KD):
                            last = pe.transpose(ring[:, bank, k * P:(k + 1) * P],
                                                raw_a[w][:, m * D + k * P:m * D + (k + 1) * P], id32[:, :])
                        last.then_inc(wt_done, 1)

                def latents():
                    pe.wait_ge(aw_loaded[3], 32)
                    for g in range(KD):
                        last = pe.transpose(ug[:, 0, g * NL:(g + 1) * NL], latr[0:NL, g * P:(g + 1) * P],
                                            id32[0:NL, 0:NL])
                    last.then_inc(lat_done, 1)

                def ternary(n):
                    if n == 0:
                        pe.wait_ge(idents, 2)
                        pe.wait_ge(lat_lo, 1)
                    pe.wait_ge(tern_ready, n + 1)
                    if n >= 2:
                        pe.wait_ge(tp_evicted, n - 1)
                    for b in range(8):
                        o = ((b % 4) * 2 + b // 4) if n < 16 else b
                        last = pe.transpose(tpb[n % 2][:, o * P:(o + 1) * P], tern[n][:, b * P:(b + 1) * P], id16[:, :])
                    last.then_inc(tp_done, 1)

                def project(w, bank, m, stop):
                    n = 0
                    for k in range(KD):
                        for a, b in ((0, 0), (0, 1), (1, 0)):
                            n += 1
                            last = pe.matmul(ring[:, bank, :], wT[w][a][:, k, m * P:(m + 1) * P], xT[b][:, k, :],
                                             start=(n == 1), stop=(stop and n == 3 * KD), skip_group_check=not stop)
                    return last

                def q(m):
                    bank = bank_of("Q", 0, m)
                    if m == 0:
                        wait(pe, x_lo, i, TT, TT)
                        if kind == "first":
                            pe.wait_ge(wt_lo, KD)
                    project(0, bank, m, True).then_inc(q_done, 1)

                def logits(t):
                    for b in range(2):
                        bank = bank_of("L", 0, 2 * t + b)
                        if t == 0:
                            wait(pe, q_lo, i, KD, 2 * b + 2)
                            if kind == "first" and b == 0:
                                pe.wait_ge(lat_lo, 1)
                        for g in (2 * b, 2 * b + 1):
                            for n, (a, c) in enumerate(((0, 0), (0, 1), (1, 0))):
                                last = pe.matmul(ring[:, bank, (g % 2) * 256:(g % 2) * 256 + 256],
                                                 qaT[a][:, g, t * P:(t + 1) * P], latL[c][:, g, :],
                                                 start=(n == 0), stop=(n == 2))
                        last.then_inc(l_done, 1)

                def pt(t):
                    wait(pe, p_ready, i, TT, t + 1)
                    for b in range(2):
                        bank = bank_of("PT", 0, 2 * t + b)
                        for k in range(4):
                            h = 8 * b + 2 * k
                            last = pe.transpose(ring[:, bank, k * P:(k + 1) * P], Pb[:, h * NL:(h + 2) * NL], id32[:, :])
                        last.then_inc(pt_done, 1)

                def vw(m):
                    bank = bank_of("VW", 0, m)
                    if m == 0 and kind == "first":
                        pe.wait_ge(wt_lo, 3 * KD)
                    project(1, bank, m, False)
                    if m == 0:
                        wait(pe, pt_lo, i, 8, 8)
                        if kind == "first":
                            pe.wait_ge(lat_lo, 2)
                    for n, (a, c) in enumerate(((0, 0), (0, 1), (1, 0))):
                        for s in range(2):
                            last = pe.matmul(ring[64 * s:64 * s + 64, bank, :], latV[a][:, 2 * m + s, :],
                                             PT[:, c, 2 * m + s, :], start=False, stop=(n == 2), skip_group_check=True)
                    last.then_inc(vw_done, 1)

                def wo(t):
                    bank = bank_of("WO", 0, t)
                    if t == 0:
                        wait(pe, a_lo, i, KD, KD)
                    n = 0
                    for k in range(KD):
                        for a, b in ((0, 0), (0, 1), (1, 0)):
                            n += 1
                            last = pe.matmul(ring[:, bank, :], qaT[a][:, k, t * P:(t + 1) * P], wT[2][b][:, k, :],
                                             start=(n == 1), stop=(n == 3 * KD))
                    last.then_inc(wo_done, 1)

                def upgate(e):
                    if e == 0:
                        wait(pe, x1_lo, j, TT, TT)
                    wait(pe, h32_ready, j, NE, e - 1)
                    for s, w in ((0, tu), (1, tg)):
                        for k in range(KD):
                            for b in range(2):
                                last = pe.matmul(ug[:, 2 * (e % 2) + s, :], w[:, k, e * P:(e + 1) * P], X1T[:, b, k, :],
                                                 start=(k == 0 and b == 0), stop=(k == KD - 1 and b == 1))
                    last.then_inc(ug_done, 1)

                def down(t):
                    bank = bank_of("DN", -1, t)
                    for e in range(NE):
                        if t == 0:
                            wait(pe, h_lo, j, NE, e + 1)
                        for a in range(2):
                            last = pe.matmul(ring[:, bank, :], hT[:, a, e, t * P:(t + 1) * P], td[:, e, :],
                                             start=(e == 0 and a == 0), stop=(e == NE - 1 and a == 1))
                    last.then_inc(dn_done, 1)

                if kind == "first":
                    pe.wait_ge(idents, 1)
                    for t in range(TT):
                        s1(0, t)
                    weights(0)
                    latents()
                if att:
                    for m in range(KD):
                        q(m)
                if ffn and att:
                    t2(-1, 2)
                    t2(-1, 3)
                if att:
                    logits(0)
                    logits(1)
                if kind == "first":
                    weights(1)
                    after = {1: [(weights, 2)], 5: [(pt, 0), (logits, 2)], 8: [(pt, 1), (logits, 3)], 11: [(pt, 2)], 14: [(pt, 3)], 15: [(vw, 0)],
                             17: [(vw, 1)], 19: [(vw, 2)], 21: [(vw, 3)],
                             23: [(s1, 1, 0), (s1, 1, 1), (wo, 0), (wo, 1), (s1, 1, 2), (s1, 1, 3), (wo, 2), (wo, 3),
                                  (t2, 0, 0), (t2, 0, 1)]}
                    for n in range(24):
                        ternary(n)
                        for f, *a in after.get(n, ()):
                            f(*a)
                    return
                for e in range(NE):
                    if ffn:
                        upgate(e)
                    if not att:
                        continue
                    if e == 5:
                        pt(0)
                        logits(2)
                    if e == 9:
                        pt(1)
                        logits(3)
                    if e == 13:
                        pt(2)
                if ffn:
                    down(0)
                if att:
                    pt(3)
                if ffn:
                    down(1)
                if att:
                    for m in range(KD):
                        vw(m)
                if nxt:
                    s1(1, 0)
                    s1(1, 1)
                if ffn:
                    down(2)
                if kind == "last":
                    for t in range(TT):
                        wo(t)
                    t2(0, 0)
                    t2(0, 1)
                    down(3)
                    t2(0, 2)
                    t2(0, 3)
                    return
                if att:
                    wo(0)
                    wo(1)
                if nxt:
                    s1(1, 2)
                    s1(1, 3)
                if ffn:
                    down(3)
                if att:
                    wo(2)
                    wo(3)
                    t2(0, 0)
                    t2(0, 1)

            bodies(pe, body)

        @block.scalar
        def _(act):
            def body(i, kind, att, ffn, nxt):
                plan = plans[kind]
                j = i - 1

                def blocks(what, c, n):
                    return ring[:, plan[(what, c, n)][0], :].rearrange("p (k b) -> p k b", k=KD)

                def s1_rows(c, t):
                    wait(act, ln1_bias, i + c, 1, 1)
                    if t < 2:
                        wait(act, t2_done, i + c - 2, TT, t + 3)
                    else:
                        wait(act, s1_done, i + c, TT, t - 1)
                    act.activation(xn[:, t % 2, :], x_in[:, t, :], ACT.Identity, scale=rs1[:, t:t + 1],
                                   bias=nb1[:, t:t + 1]).then_inc(xn1_ready, 1)

                def s1_hi(c, t):
                    wait(act, s1_done, i + c, TT, t + 1)
                    wait(act, vw_done, i + c, KD, 0)
                    act.activation(xT[0][:, :, t * P:(t + 1) * P], blocks("S1", c, t), ACT.Copy).then_inc(x_hi, 1)

                def t2_rows(c, t):
                    wait(act, ln2_bias, i + c, TT, t + 1)
                    if t >= 2:
                        wait(act, t2_done, i + c, TT, t - 1)
                    elif nxt:
                        wait(act, s1_done, i + 1, TT, t + 3)
                    else:
                        wait(act, t2_done, i - 1, TT, t + 3)
                    act.activation(xn[:, t % 2, :], residual(kind == "last" and c == 0)[:, t, :], ACT.Identity, scale=rsx[:, t % 2:t % 2 + 1],
                                   bias=nbx[:, t % 2:t % 2 + 1]).then_inc(xn2_ready, 1)

                def t2_hi(c, t):
                    wait(act, t2_done, i + c, TT, t + 1)
                    wait(act, ug_done, i + c, NE, 0)
                    act.activation(X1T[:, 0, :, t * P:(t + 1) * P], blocks("T2", c, t), ACT.Copy).then_inc(x1_hi, 1)

                def weights_hi(w):
                    if w < 2:
                        act.wait_ge(scales, w + 1)
                    for m in range(KD):
                        act.wait_ge(wt_done, KD * w + m + 1)
                        act.activation(wT[w][0][:, :, m * P:(m + 1) * P], blocks("WT", 0, KD * w + m), ACT.Copy,
                                       scale=up[:, WSCALE[w]:WSCALE[w] + 1]).then_inc(wt_hi, 1)

                def latL_hi():
                    act.wait_ge(lat_done, 1)
                    act.wait_ge(zeroed, 1)
                    for hh in range(4):
                        rows = slice(HD * hh, HD * hh + HD)
                        last = act.activation(latL[0][rows, :, hh * NL:(hh + 1) * NL],
                                              ug[rows, 0, 0:KD * NL].rearrange("p (g l) -> p g l", g=KD), ACT.Copy,
                                              scale=up[rows, 1:2])
                    last.then_inc(lat_hi, 1)

                def latV_hi():
                    for hh in range(2):
                        rows = slice(NL * hh, NL * hh + NL)
                        last = act.activation(latV[0][rows, :, hh * HD:(hh + 1) * HD],
                                              latr[rows, :].rearrange("p (j h d) -> p j h d", h=2, d=HD)[:, :, hh, :],
                                              ACT.Copy, scale=up[rows, 2:3])
                    last.then_inc(lat_hi, 1)

                def abs_sum(*pieces):
                    for n in pieces:
                        act.wait_ge(w_loaded[n], 16)
                        before = n - sum(m < n for m in ASUM_DVE)
                        if before:
                            act.wait_ge(asum_done, before)
                        act.activation(junk, stages[n // 8][n % 8], ACT.Abs, accum_out=asum[:, n:n + 1]).then_inc(asum_done, 1)

                def evict_ternary(n):
                    act.wait_ge(tp_done, n + 1)
                    w, q = n // 8, n % 8
                    if w < 2:
                        dst = (tu, tg)[w][:, :, 256 * q:256 * q + 256]
                        src = tpb[n % 2].rearrange("p (k e) -> p k e", k=KD)
                    else:
                        dst = td[:, 8 * (q % 2):8 * (q % 2) + 8, (q // 2) * P:(q // 2 + 1) * P]
                        src = tpb[n % 2].rearrange("p (j d) -> p j d", j=8)
                    act.activation(dst, src, ACT.Copy).then_inc(tp_evicted, 1)

                def q(m):
                    wait(act, q_done, i, KD, m + 1)
                    if m < 2:
                        wait(act, a_lo, i - 1, KD, m + 3)
                    else:
                        wait(act, q_lo, i, KD, m - 1)
                    act.activation(p32[:, m % 2, :], ring[:, plan[("Q", 0, m)][0], :], ACT.Identity,
                                   scale=PROJ, bias=bqs[:, m:m + 1]).then_inc(q32_ready, 1)
                    wait(act, q32_ready, i, KD, m + 1)
                    wait(act, wo_done, i, TT, 0)
                    act.activation(qaT[0][:, m, :], p32[:, m % 2, :], ACT.Copy).then_inc(q_hi, 1)

                def logits(t):
                    for b in range(2):
                        wait(act, l_done, i, 8, 2 * t + b + 1)
                        if b == 0:
                            wait(act, p_ready, i, TT, t - 1)
                        act.activation(Lb[:, t % 2, 8 * b:8 * b + 8, 0:NL],
                                       ring[:, plan[("L", 0, 2 * t + b)][0], :].rearrange("p (h l) -> p h l", h=8),
                                       ACT.Copy, scale=clo[:, 0:1]).then_inc(l_ready, 1)

                def exp4(t):
                    wait(act, d4_ready, i, TT, t + 1)
                    act.activation(d4[:, t % 2, :, :], d4[:, t % 2, :, :], ACT.Exp).then_inc(e4_ready, 1)

                def exps(t):
                    wait(act, shifted, i, TT, t + 1)
                    act.activation(Lb[:, t % 2, :, 0:NL], Lb[:, t % 2, :, 0:NL], ACT.Exp).then_inc(e_ready, 1)

                def pt(t):
                    for b in range(2):
                        wait(act, pt_done, i, 8, 2 * t + b + 1)
                        wait(act, vw_done, i, KD, 0)
                        act.activation(PT[:, 0, 4 * b:4 * b + 4, t * P:(t + 1) * P], blocks("PT", 0, 2 * t + b),
                                       ACT.Copy, scale=PS).then_inc(pt_hi, 1)

                def vw(m):
                    wait(act, vw_done, i, KD, m + 1)
                    if m < 2:
                        wait(act, q_lo, i, KD, m + 3)
                    else:
                        wait(act, a_lo, i, KD, m - 1)
                    act.activation(p32[:, m % 2, :], ring[:, plan[("VW", 0, m)][0], :], ACT.Identity,
                                   scale=PROJ, bias=bvs[:, m:m + 1]).then_inc(a32_ready, 1)
                    wait(act, a32_ready, i, KD, m + 1)
                    wait(act, l_done, i, 8, 8)
                    act.activation(qaT[0][:, m, :], p32[:, m % 2, :], ACT.Copy).then_inc(a_hi, 1)

                def tanh(e):
                    wait(act, ug_done, j, NE, e + 1)
                    wait(act, h32_ready, j, NE, e - 1)
                    act.activation(ugt[:, e % 2, :], ug[:, 2 * (e % 2), :], ACT.Tanh, scale=cu[:, 0:1]).then_inc(tanh_ready, 1)

                def hidden_hi(e):
                    wait(act, h32_ready, j, NE, e + 1)
                    if e == 0:
                        wait(act, dn_done, j, TT, 0)
                    act.activation(hT[:, 0, e, :], ugt[:, 2 + e % 2, :], ACT.Copy).then_inc(h_hi, 1)

                def out_rows(t):
                    wait(act, f_sum, j, TT, t + 1)
                    buf = residual(kind == "tail")[:, t, :]
                    act.activation(buf, buf, ACT.Identity, bias=nbf[:, t % 2:t % 2 + 1]).then_inc(out_ready, 1)

                if kind == "first":
                    s1_rows(0, 0)
                    s1_rows(0, 1)
                    for t in range(TT):
                        s1_hi(0, t)
                        if t < 2:
                            s1_rows(0, t + 2)
                    weights_hi(0)
                    latL_hi()
                    abs_sum(0, 1)
                if att:
                    for m in range(KD):
                        q(m)
                        if kind == "first" and m == 1:
                            abs_sum(2, 3)
                        if ffn and m == 1:
                            t2_rows(-1, 2)
                            t2_rows(-1, 3)
                if ffn and att:
                    t2_hi(-1, 2)
                    t2_hi(-1, 3)
                if att:
                    logits(0)
                    logits(1)
                if kind == "first":
                    weights_hi(1)
                    after = {0: [(exp4, 0), (abs_sum, 8)], 1: [(exps, 0), (abs_sum, 9)], 2: [(abs_sum, 10, 11), (weights_hi, 2), (latV_hi,)],
                             3: [(abs_sum, 12, 13)], 4: [(abs_sum, 14, 15)], 5: [(exp4, 1)], 6: [(pt, 0), (logits, 2), (exps, 1)],
                             8: [(exp4, 2), (abs_sum, 16, 17)], 9: [(pt, 1), (logits, 3), (exps, 2), (abs_sum, 18, 19)],
                             10: [(abs_sum, 20, 21)], 11: [(exp4, 3), (abs_sum, 22, 23)], 12: [(pt, 2), (exps, 3)],
                             15: [(pt, 3)], 16: [(vw, 0)], 18: [(vw, 1), (s1_rows, 1, 0)], 20: [(vw, 2), (s1_rows, 1, 1)],
                             22: [(vw, 3)],
                             24: [(s1_hi, 1, 0), (s1_rows, 1, 2), (s1_hi, 1, 1), (s1_rows, 1, 3), (s1_hi, 1, 2), (s1_hi, 1, 3),
                                  (t2_rows, 0, 0), (t2_rows, 0, 1)]}
                    for n in range(25):
                        if n:
                            evict_ternary(n - 1)
                        for f, *a in after.get(n, ()):
                            f(*a)
                    t2_hi(0, 0)
                    t2_hi(0, 1)
                    return
                for e in range(NE):
                    if ffn:
                        tanh(e)
                        if e:
                            hidden_hi(e - 1)
                    if not att:
                        continue
                    if e in (2, 4, 8, 12):
                        exp4((2, 4, 8, 12).index(e))
                    if e in (3, 6, 10, 14):
                        exps((3, 6, 10, 14).index(e))
                    if e == 5:
                        pt(0)
                        logits(2)
                    if e == 9:
                        pt(1)
                        logits(3)
                    if e == 13:
                        pt(2)
                if ffn:
                    hidden_hi(NE - 1)
                if nxt:
                    s1_rows(1, 0)
                    s1_rows(1, 1)
                if ffn:
                    out_rows(0)
                if att:
                    pt(3)
                if ffn:
                    out_rows(1)
                if att:
                    for m in range(KD):
                        vw(m)
                if nxt:
                    s1_hi(1, 0)
                    s1_rows(1, 2)
                    s1_hi(1, 1)
                    s1_rows(1, 3)
                if ffn:
                    out_rows(2)
                if nxt:
                    s1_hi(1, 2)
                    s1_hi(1, 3)
                if kind != "last":
                    out_rows(3)
                if att:
                    t2_rows(0, 0)
                    t2_rows(0, 1)
                    t2_hi(0, 0)
                    t2_hi(0, 1)
                if kind == "last":
                    t2_rows(0, 2)
                    t2_rows(0, 3)
                    t2_hi(0, 2)
                    t2_hi(0, 3)
                    out_rows(3)

            bodies(act, body)

        @block.gpsimd
        def _(pool):
            pool.memset(id32[:, :], 0.0).then_inc(id_zeroed, 1)
            pool.memset(nh[:, :], -0.5).then_inc(consts, 1)
            pool.wait_ge(id_zeroed, 1)
            pool.affine_select(out=id32[:, :], in_=id32[:, :], compare_op=ALU.not_equal, fill=1.0, base=0,
                               pattern=[[-1, P]], channel_multiplier=1).then_inc(idents, 1)
            for s in range(2):
                pool.memset(latV[s][:, :, :], 0.0)
                pool.memset(latL[s][:, :, :], 0.0)
            pool.memset(Lb[:, :, :, NL:LW], PAD).then_inc(zeroed, 1)
            pool.wait_ge(consts, 1)

            def rstd(dst, src, width, var_ready, c, per, n, done):
                wait(pool, var_ready, c, per, n)
                pool.tensor_tensor(dst, src, nh[:, 0:width], ALU.pow).then_inc(done, 1)

            def ln1_rstd_of(c):
                rstd(rs1[:, :], va1[:, :], TT, ln1_var, c, 1, 1, ln1_rstd)

            ln1_rstd_of(0)

            def all_maxima(g):
                pool.wait_ge(mg_ready, g + 1)
                pool.partition_all_reduce(ma[:, 2 * g:2 * g + 2], mg[:, 2 * g:2 * g + 2], P, RMAX).then_inc(ma_ready, 1)

            all_maxima(0)

            def all_sum(w):
                pool.wait_ge(tot_ready, w + 1)
                pool.partition_all_reduce(tota[:, w:w + 1], tot[:, w:w + 1], P, RADD).then_inc(tota_ready, 1)

            def below(n):
                w, q = n // 8, n % 8
                if n in BELOW_DVE:
                    return
                pool.wait_ge(tern_scale, w + 1)
                slot_free(pool, n)
                pool.tensor_scalar(tern[n], stages[w][q], nhw[:, w:w + 1], None, ALU.is_lt).then_inc(below_ready, 1)

            def body(i, kind, att, ffn, nxt):
                j = i - 1

                def low_q(m):
                    wait(pool, q_hi, i, KD, m + 1)
                    pool.tensor_tensor(qaT[1][:, m, :], p32[:, m % 2, :], qaT[0][:, m, :], ALU.subtract).then_inc(q_lo, 1)

                def low_a(m):
                    wait(pool, a_hi, i, KD, m + 1)
                    pool.tensor_tensor(qaT[1][:, m, :], p32[:, m % 2, :], qaT[0][:, m, :], ALU.subtract).then_inc(a_lo, 1)

                def shift(t):
                    wait(pool, replaced, i, TT, t + 1)
                    buf = Lb[:, t % 2, :, 0:NL]
                    pool.tensor_tensor(buf, buf, v8[:, t % 2, :, 0:1].broadcast_to([P, H, NL]), ALU.subtract).then_inc(shifted, 1)

                def normalise(t):
                    wait(pool, recip_ready, i, TT, t + 1)
                    wait(pool, p_raw, i, TT, t + 1)
                    wait(pool, pt_done, i, 8, 2 * t)
                    pool.tensor_tensor(Pb.rearrange("p (h l) -> p h l", h=H), Lb[:, t % 2, :, 0:NL],
                                       r4[:, t % 2, :].rearrange("p (h a) -> p h a", a=1).broadcast_to([P, H, NL]),
                                       ALU.mult).then_inc(p_ready, 1)

                def hidden_lo(e):
                    wait(pool, h_hi, j, NE, e + 1)
                    pool.tensor_tensor(hT[:, 1, e, :], ugt[:, 2 + e % 2, :], hT[:, 0, e, :], ALU.subtract).then_inc(h_lo, 1)

                def rstd_y(t):
                    rstd(rsy[:, t % 2:t % 2 + 1], vay[:, t % 2:t % 2 + 1], 1, y_var, i, TT, t + 1, y_rstd)

                def rstd_x(c, t):
                    rstd(rsx[:, t % 2:t % 2 + 1], vax[:, t % 2:t % 2 + 1], 1, ln2_var, i + c, TT, t + 1, ln2_rstd)

                def rstd_f(t):
                    rstd(rsf[:, t % 2:t % 2 + 1], vaf[:, t % 2:t % 2 + 1], 1, f_var, j, TT, t + 1, f_rstd)

                if att:
                    for m in range(KD):
                        low_q(m)
                        if ffn and m == 0:
                            rstd_x(-1, 2)
                            rstd_x(-1, 3)
                        if kind == "first" and m == 1:
                            all_maxima(1)
                if kind == "first":
                    all_sum(0)
                    after = {0: [(shift, 0)], 4: [(normalise, 0)], 6: [(shift, 1)], 7: [(all_sum, 1)], 8: [(normalise, 1)],
                             10: [(shift, 2)], 12: [(normalise, 2)], 14: [(shift, 3), (normalise, 3), (all_sum, 2), (ln1_rstd_of, i + 1)],
                             23: [(low_a, 0), (low_a, 1), (low_a, 2), (low_a, 3), (rstd_y, 0), (rstd_y, 1),
                                  (rstd_x, 0, 0), (rstd_x, 0, 1), (rstd_y, 2), (rstd_y, 3)]}
                    for n in range(24):
                        below(n)
                        for f, *a in after.get(n, ()):
                            f(*a)
                    return
                for e in range(NE):
                    if ffn:
                        hidden_lo(e)
                    if not att:
                        continue
                    if e in (1, 4, 8, 12):
                        shift((1, 4, 8, 12).index(e))
                    if e in (2, 6, 10, 14):
                        normalise((2, 6, 10, 14).index(e))
                if nxt:
                    ln1_rstd_of(i + 1)
                if ffn:
                    rstd_f(0)
                    rstd_f(1)
                if att:
                    for m in range(KD):
                        low_a(m)
                if ffn:
                    rstd_f(2)
                if att:
                    rstd_y(0)
                    rstd_y(1)
                    rstd_x(0, 0)
                    rstd_x(0, 1)
                if kind != "last":
                    rstd_f(3)
                if att:
                    rstd_y(2)
                    rstd_y(3)
                if kind == "last":
                    rstd_x(0, 2)
                    rstd_x(0, 3)
                    rstd_f(3)

            bodies(pool, body)

        @block.vector
        def _(dve):
            def maxima(src, s, v, col):
                dve.wait_ge(aw_loaded[s], v)
                dve.tensor_reduce(mx[:, col:col + 1], src, AX.X, ALU.max, apply_absolute_value=True).then_inc(mx_ready, 1)

            def powers(g):
                cols, one = slice(2 * g, 2 * g + 2), slice(g, g + 1)
                at = 6 * g
                dve.wait_ge(ma_ready, g + 1)
                dve.tensor_scalar(sc[:, cols], ma[:, cols], TINY, None, ALU.max).then_inc(sc_step, 1)
                dve.wait_ge(sc_step, at + 1)
                dve.tensor_scalar(sc[:, cols].bitcast(U32), sc[:, cols].bitcast(U32), 0x7F800000, None,
                                  ALU.bitwise_and).then_inc(sc_step, 1)
                dve.wait_ge(sc_step, at + 2)
                dve.reciprocal(inv[:, cols], sc[:, cols]).then_inc(sc_step, 1)
                dve.tensor_tensor(clo[:, one], sc[:, 2 * g:2 * g + 1], sc[:, 2 * g + 1:2 * g + 2], ALU.mult).then_inc(sc_step, 1)
                dve.wait_ge(sc_step, at + 4)
                dve.tensor_scalar(up[:, cols], inv[:, cols], WS, None, ALU.mult)
                dve.tensor_scalar(upb[:, one], inv[:, 2 * g:2 * g + 1], AS, None, ALU.mult).then_inc(sc_step, 1)
                dve.tensor_scalar(clo[:, one], clo[:, one], (float(HD) ** -0.5, 1.0)[g] / (AS * WS), None, ALU.mult).then_inc(sc_step, 1)
                dve.wait_ge(sc_step, at + 6)
                dve.tensor_scalar((bqs, bvs)[g][:, :], (bqc, bvc)[g][:, :], upb[:, one], None, ALU.mult).then_inc(scales, 1)

            def abs_sum(n):
                dve.wait_ge(w_loaded[n], 16)
                dve.tensor_reduce(asum[:, n:n + 1], stages[n // 8][n % 8], AX.X, ALU.add, apply_absolute_value=True).then_inc(own_asum, 1)

            def tern_total(w):
                dve.wait_ge(asum_done, 8 * w + 8 - len(ASUM_DVE))
                dve.wait_ge(own_asum, len(ASUM_DVE))
                dve.reduce_sum(tot[:, w:w + 1], asum[:, 8 * w:8 * w + 8], AX.X).then_inc(tot_ready, 1)

            def tern_scale_of(w):
                dve.wait_ge(tota_ready, w + 1)
                dve.tensor_scalar(sw[:, w:w + 1], tota[:, w:w + 1], 1.0 / (E * D), QEPS, ALU.mult, ALU.add).then_inc(tern_step, 1)
                dve.wait_ge(tern_step, w + 1)
                dve.tensor_scalar(hw[:, w:w + 1], sw[:, w:w + 1], 0.5, None, ALU.mult)
                dve.tensor_scalar(nhw[:, w:w + 1], sw[:, w:w + 1], -0.5, None, ALU.mult).then_inc(tern_scale, 1)
                dve.wait_ge(tern_scale, w + 1)

            def ternarise(n):
                w, q = n // 8, n % 8
                if n in BELOW_DVE:
                    slot_free(dve, n)
                    dve.tensor_scalar(tern[n], stages[w][q], nhw[:, w:w + 1], None, ALU.is_lt).then_inc(own_below, 1)
                    dve.wait_ge(own_below, BELOW_DVE.index(n) + 1)
                else:
                    dve.wait_ge(below_ready, n + 1 - sum(m < n for m in BELOW_DVE))
                dve.scalar_tensor_tensor(out=tern[n], in0=stages[w][q], scalar=hw[:, w:w + 1], in1=tern[n],
                                         op0=ALU.is_gt, op1=ALU.subtract).then_inc(tern_ready, 1)

            def ffn_scales():
                dve.tensor_scalar(cu[:, :], sw[:, 0:1], 0.5 / XS, None, ALU.mult)
                dve.tensor_tensor(cf[:, 0:1], sw[:, 0:1], sw[:, 1:2], ALU.mult).then_inc(tern_step, 1)
                dve.wait_ge(tern_step, 4)
                dve.scalar_tensor_tensor(out=cf[:, 1:2], in0=cf[:, 0:1], scalar=0.5 / (XS * XS * HS), in1=sw[:, 2:3],
                                         op0=ALU.mult, op1=ALU.mult).then_inc(tern_step, 1)
                dve.wait_ge(tern_step, 5)

            def body(i, kind, att, ffn, nxt):
                plan = plans[kind]
                j = i - 1

                def blocks(what, c, n):
                    return ring[:, plan[(what, c, n)][0], :].rearrange("p (k b) -> p k b", k=KD)

                def ln1_stat(c):
                    wait(dve, x_in_loaded, i + c, 16, 16)
                    for t in range(TT):
                        last = dve.bn_stats(st1[:, t, :], x_in[:, t, :])
                    last.then_inc(ln1_stats, 1)
                    wait(dve, ln1_stats, i + c, 1, 1)
                    dve.sem_inc(own_wait, 1)
                    for t in range(TT):
                        last = dve.bn_aggr(mv1[:, t, :], st1[:, t, :])
                    last.then_inc(ln1_mean, 1)
                    wait(dve, ln1_mean, i + c, 1, 1)
                    dve.tensor_scalar(va1[:, :], mv1[:, :, 1], XS ** -2, EPS * XS ** -2, ALU.mult, ALU.add).then_inc(ln1_var, 1)

                def ln1_biases(c):
                    wait(dve, ln1_rstd, i + c, 1, 1)
                    dve.scalar_tensor_tensor(out=nb1[:, :], in0=mv1[:, :, 0], scalar=-1.0, in1=rs1[:, :],
                                             op0=ALU.mult, op1=ALU.mult).then_inc(ln1_bias, 1)

                def s1_lo(c, t):
                    wait(dve, x_hi, i + c, TT, t + 1)
                    dve.tensor_tensor(xT[1][:, :, t * P:(t + 1) * P], blocks("S1", c, t),
                                      xT[0][:, :, t * P:(t + 1) * P], ALU.subtract).then_inc(x_lo, 1)

                def weights_lo(w):
                    for m in range(KD):
                        dve.wait_ge(wt_hi, KD * w + m + 1)
                        dve.scalar_tensor_tensor(out=wT[w][1][:, :, m * P:(m + 1) * P], in0=blocks("WT", 0, KD * w + m),
                                                 scalar=up[:, WSCALE[w]:WSCALE[w] + 1],
                                                 in1=wT[w][0][:, :, m * P:(m + 1) * P],
                                                 op0=ALU.mult, op1=ALU.subtract).then_inc(wt_lo, 1)

                def latL_lo():
                    dve.wait_ge(lat_hi, 1)
                    for hh in range(4):
                        rows = slice(HD * hh, HD * hh + HD)
                        last = dve.scalar_tensor_tensor(out=latL[1][rows, :, hh * NL:(hh + 1) * NL],
                                                        in0=ug[rows, 0, 0:KD * NL].rearrange("p (g l) -> p g l", g=KD),
                                                        scalar=up[rows, 1:2], in1=latL[0][rows, :, hh * NL:(hh + 1) * NL],
                                                        op0=ALU.mult, op1=ALU.subtract)
                    last.then_inc(lat_lo, 1)

                def latV_lo():
                    dve.wait_ge(lat_hi, 2)
                    for hh in range(2):
                        rows = slice(NL * hh, NL * hh + NL)
                        last = dve.scalar_tensor_tensor(out=latV[1][rows, :, hh * HD:(hh + 1) * HD],
                                                        in0=latr[rows, :].rearrange("p (j h d) -> p j h d", h=2, d=HD)[:, :, hh, :],
                                                        scalar=up[rows, 2:3], in1=latV[0][rows, :, hh * HD:(hh + 1) * HD],
                                                        op0=ALU.mult, op1=ALU.subtract)
                    last.then_inc(lat_lo, 1)

                def t2_lo(c, t):
                    wait(dve, x1_hi, i + c, TT, t + 1)
                    dve.tensor_tensor(X1T[:, 1, :, t * P:(t + 1) * P], blocks("T2", c, t),
                                      X1T[:, 0, :, t * P:(t + 1) * P], ALU.subtract).then_inc(x1_lo, 1)

                def hidden(e):
                    wait(dve, tanh_ready, j, NE, e + 1)
                    dve.scalar_tensor_tensor(out=ugt[:, e % 2, :], in0=ugt[:, e % 2, :], scalar=1.0,
                                             in1=ug[:, 2 * (e % 2), :], op0=ALU.add, op1=ALU.mult).then_inc(t1_ready, 1)
                    wait(dve, t1_ready, j, NE, e + 1)
                    wait(dve, h_lo, j, NE, e - 1)
                    dve.scalar_tensor_tensor(out=ugt[:, 2 + e % 2, :], in0=ugt[:, e % 2, :], scalar=HS,
                                             in1=ug[:, 2 * (e % 2) + 1, :], op0=ALU.mult, op1=ALU.mult).then_inc(h32_ready, 1)

                def maxes(t, b):
                    wait(dve, l_ready, i, 8, 2 * t + b + 1)
                    if b == 0:
                        wait(dve, shifted, i, TT, t - 1)
                    dve.sem_inc(own_wait, 1)
                    for h in range(8 * b, 8 * b + 8):
                        last = dve.max(v8[:, t % 2, h, :], Lb[:, t % 2, h, 0:NL])
                    if b:
                        last.then_inc(top8, 1)

                def slots(t):
                    wait(dve, top8, i, TT, t + 1)
                    dve.memset(v8[:, t % 2, :, TOPK:8], PAD).then_inc(v8_ready, 1)
                    wait(dve, recip_ready, i, TT, t - 1)
                    dve.tensor_tensor(d4[:, t % 2, :, :], v8[:, t % 2, :, 0:TOPK],
                                      v8[:, t % 2, :, 0:1].broadcast_to([P, H, TOPK]), ALU.subtract).then_inc(d4_ready, 1)

                def replace(t, b):
                    wait(dve, v8_ready, i, TT, t + 1)
                    wait(dve, p_raw, i, TT, t)
                    dve.sem_inc(own_wait, 1)
                    for h in range(8 * b, 8 * b + 8):
                        last = dve.match_replace(Lr[:, h, :], v8[:, t % 2, h, :], Lb[:, t % 2, h, :], HIT)
                    if b:
                        last.then_inc(replaced, 1)

                def sums(t):
                    wait(dve, e4_ready, i, TT, t + 1)
                    dve.tensor_reduce(s4[:, t % 2, :], d4[:, t % 2, :, :], AX.X, ALU.add).then_inc(sum_ready, 1)
                    wait(dve, sum_ready, i, TT, t + 1)
                    wait(dve, p_ready, i, TT, t - 1)
                    dve.reciprocal(r4[:, t % 2, :], s4[:, t % 2, :]).then_inc(recip_ready, 1)

                def select(t):
                    wait(dve, e_ready, i, TT, t + 1)
                    buf = Lb[:, t % 2, :, 0:NL]
                    dve.scalar_tensor_tensor(out=buf, in0=Lr[:, :, 0:NL], scalar=HIT, in1=buf,
                                             op0=ALU.is_equal, op1=ALU.mult).then_inc(p_raw, 1)

                def pt_low(t):
                    for b in range(2):
                        wait(dve, pt_hi, i, 8, 2 * t + b + 1)
                        dve.scalar_tensor_tensor(out=PT[:, 1, 4 * b:4 * b + 4, t * P:(t + 1) * P],
                                                 in0=blocks("PT", 0, 2 * t + b), scalar=PS,
                                                 in1=PT[:, 0, 4 * b:4 * b + 4, t * P:(t + 1) * P],
                                                 op0=ALU.mult, op1=ALU.subtract).then_inc(pt_lo, 1)

                def f_a(t):
                    s = t % 2
                    wait(dve, dn_done, j, TT, t + 1)
                    dve.bn_stats(stf[:, s, :], ring[:, plan[("DN", -1, t)][0], :]).then_inc(f_stats, 1)
                    wait(dve, f_stats, j, TT, t + 1)
                    dve.sem_inc(own_wait, 1)
                    dve.bn_aggr(mvf[:, s, :], stf[:, s, :]).then_inc(f_mean, 1)
                    wait(dve, f_mean, j, TT, t + 1)
                    dve.tensor_scalar(vaf[:, s:s + 1], mvf[:, s, 1:2], cf[:, 1:2], cf[:, 1:2], ALU.mult, ALU.mult).then_inc(f_varc, 1)
                    wait(dve, f_varc, j, TT, t + 1)
                    dve.tensor_scalar(vaf[:, s:s + 1], vaf[:, s:s + 1], EPS, None, ALU.add).then_inc(f_var, 1)

                def f_b(t):
                    s = t % 2
                    wait(dve, f_rstd, j, TT, t + 1)
                    wait(dve, out_ready, j, TT, t - 1)
                    dve.tensor_tensor(rcf[:, s:s + 1], rsf[:, s:s + 1], cf[:, 1:2], ALU.mult).then_inc(f_scale, 1)
                    wait(dve, f_scale, j, TT, t + 1)
                    dve.scalar_tensor_tensor(out=nbf[:, s:s + 1], in0=mvf[:, s, 0:1], scalar=rcf[:, s:s + 1],
                                             in1=(nby_last if kind == "tail" else nby)[:, t:t + 1],
                                             op0=ALU.mult, op1=ALU.subtract, reverse1=True).then_inc(f_bias, 1)
                    buf = residual(kind == "tail")[:, t, :]
                    dve.scalar_tensor_tensor(out=buf, in0=ring[:, plan[("DN", -1, t)][0], :], scalar=rcf[:, s:s + 1], in1=buf, op0=ALU.mult, op1=ALU.add).then_inc(f_sum, 1)

                def y_a(t):
                    s = t % 2
                    wait(dve, wo_done, i, TT, t + 1)
                    if kind == "first" and t == 0:
                        dve.wait_ge(aw_loaded[6], 16)
                        dve.wait_ge(lat_lo, 2)
                    wait(dve, x1_ready, i, TT, t - 1)
                    dve.scalar_tensor_tensor(out=row[:, s, :], in0=ring[:, plan[("WO", 0, t)][0], :], scalar=clo[:, 1:2],
                                             in1=bo_b[:, :], op0=ALU.mult, op1=ALU.add).then_inc(y_ready, 1)
                    wait(dve, y_ready, i, TT, t + 1)
                    dve.bn_stats(sty[:, s, :], row[:, s, :]).then_inc(y_stats, 1)
                    wait(dve, y_stats, i, TT, t + 1)
                    dve.sem_inc(own_wait, 1)
                    dve.bn_aggr(mvy[:, s, :], sty[:, s, :]).then_inc(y_mean, 1)
                    wait(dve, y_mean, i, TT, t + 1)
                    dve.tensor_scalar(vay[:, s:s + 1], mvy[:, s, 1:2], EPS, None, ALU.add).then_inc(y_var, 1)

                def y_b(t):
                    s = t % 2
                    wait(dve, y_rstd, i, TT, t + 1)
                    if kind == "last":
                        wait(dve, xn1_ready, i, TT, TT)
                    else:
                        wait(dve, x_res_loaded[t], i, 16, 16)
                    buf = residual(kind == "last")[:, t, :]
                    dve.scalar_tensor_tensor(out=buf, in0=row[:, s, :], scalar=rsy[:, s:s + 1], in1=buf, op0=ALU.mult, op1=ALU.add).then_inc(x1_ready, 1)
                    dve.tensor_scalar((nby_last if kind == "last" else nby)[:, t:t + 1], mvy[:, s, 0:1], rsy[:, s:s + 1], -1.0, ALU.mult, ALU.mult)
                    wait(dve, x1_ready, i, TT, t + 1)
                    dve.bn_stats(stx[:, s, :], buf).then_inc(ln2_stats, 1)
                    wait(dve, ln2_stats, i, TT, t + 1)
                    dve.sem_inc(own_wait, 1)
                    dve.bn_aggr(mvx[:, s, :], stx[:, s, :]).then_inc(ln2_mean, 1)
                    wait(dve, ln2_mean, i, TT, t + 1)
                    dve.tensor_scalar(vax[:, s:s + 1], mvx[:, s, 1:2], XS ** -2, EPS * XS ** -2, ALU.mult, ALU.add).then_inc(ln2_var, 1)

                def y_c(t):
                    s = t % 2
                    wait(dve, ln2_rstd, i, TT, t + 1)
                    wait(dve, xn2_ready, i, TT, t - 1)
                    dve.tensor_scalar(nbx[:, s:s + 1], mvx[:, s, 0:1], rsx[:, s:s + 1], -1.0, ALU.mult, ALU.mult).then_inc(ln2_bias, 1)

                if kind == "first":
                    ln1_stat(0)
                    maxima(latr, 3, 32, 2)
                    maxima(bqc[:, :], 4, 16, 1)
                    maxima(raw_a[0], 0, 16, 0)
                    dve.wait_ge(mx_ready, 3)
                    dve.tensor_copy(mg[:, 1:2], mx[:, 2:3])
                    dve.tensor_tensor(mg[:, 0:1], mx[:, 0:1], mx[:, 1:2], ALU.max).then_inc(mg_ready, 1)
                    ln1_biases(0)
                    dve.wait_ge(idents, 1)
                    dve.tensor_copy(id16[:, :], id32[:, :]).then_inc(idents, 1)
                    powers(0)
                    for t in range(TT):
                        s1_lo(0, t)
                    weights_lo(0)
                    latL_lo()
                    maxima(bvc[:, :], 5, 16, 4)
                    maxima(raw_a[1], 1, 16, 3)
                    maxima(raw_a[2], 2, 16, 5)
                    dve.wait_ge(mx_ready, 6)
                    dve.tensor_copy(mg[:, 3:4], mx[:, 5:6])
                    dve.tensor_reduce(mg[:, 2:3], mx[:, 2:5], AX.X, ALU.max).then_inc(mg_ready, 1)
                    for n in ASUM_DVE:
                        abs_sum(n)
                    powers(1)
                if ffn and att:
                    t2_lo(-1, 2)
                    t2_lo(-1, 3)
                if kind == "first":
                    tern_total(0)
                    tern_scale_of(0)
                    after = {0: [(maxes, 0, 0), (maxes, 0, 1), (slots, 0), (replace, 0, 0), (replace, 0, 1)],
                             1: [(weights_lo, 1)],
                             2: [(maxes, 1, 0), (sums, 0), (select, 0)], 3: [(weights_lo, 2), (latV_lo,), (maxes, 1, 1), (slots, 1)],
                             4: [(replace, 1, 0), (replace, 1, 1)], 5: [(tern_total, 1)],
                             6: [(pt_low, 0), (maxes, 2, 0), (maxes, 2, 1), (sums, 1), (select, 1), (slots, 2)],
                             7: [(replace, 2, 0), (replace, 2, 1), (tern_scale_of, 1)],
                             9: [(pt_low, 1), (maxes, 3, 0), (maxes, 3, 1), (sums, 2), (select, 2), (slots, 3)],
                             10: [(replace, 3, 0), (replace, 3, 1)], 12: [(pt_low, 2), (sums, 3), (select, 3)],
                             13: [(tern_total, 2)], 14: [(ln1_stat, 1)], 15: [(pt_low, 3), (tern_scale_of, 2), (ln1_biases, 1)],
                             23: [(s1_lo, 1, 0), (s1_lo, 1, 1), (y_a, 0), (y_a, 1), (s1_lo, 1, 2), (s1_lo, 1, 3),
                                  (y_b, 0), (y_b, 1), (y_c, 0), (y_c, 1), (y_a, 2), (y_a, 3)]}
                    for n in range(24):
                        ternarise(n)
                        for f, *a in after.get(n, ()):
                            f(*a)
                    ffn_scales()
                    t2_lo(0, 0)
                    t2_lo(0, 1)
                    y_b(2)
                    y_b(3)
                    y_c(2)
                    y_c(3)
                    return
                AFTER = {0: [(maxes, 0, 0)], 1: [(maxes, 0, 1), (slots, 0), (replace, 0, 0)],
                         2: [(replace, 0, 1), (maxes, 1, 0)], 3: [(sums, 0), (select, 0), (maxes, 1, 1), (slots, 1)],
                         4: [(replace, 1, 0)], 5: [(replace, 1, 1), (pt_low, 0)],
                         6: [(sums, 1), (select, 1), (maxes, 2, 0)], 7: [(maxes, 2, 1), (slots, 2)],
                         8: [(replace, 2, 0)], 9: [(replace, 2, 1), (pt_low, 1)],
                         10: [(sums, 2), (select, 2)], 11: [(maxes, 3, 0), (maxes, 3, 1), (slots, 3)],
                         12: [(replace, 3, 0)], 13: [(replace, 3, 1), (pt_low, 2)],
                         14: [(sums, 3), (select, 3)], 15: []}
                for e in range(NE):
                    if ffn:
                        hidden(e)
                    if att:
                        for f, *a in AFTER[e]:
                            f(*a)
                if nxt:
                    ln1_stat(1)
                    ln1_biases(1)
                if ffn:
                    f_a(0)
                    f_b(0)
                if att:
                    pt_low(3)
                if ffn:
                    f_a(1)
                    f_b(1)
                if nxt:
                    s1_lo(1, 0)
                    s1_lo(1, 1)
                if ffn:
                    f_a(2)
                    f_b(2)
                if att:
                    y_a(0)
                    y_a(1)
                    y_b(0)
                    y_b(1)
                    y_c(0)
                    y_c(1)
                if nxt:
                    s1_lo(1, 2)
                    s1_lo(1, 3)
                if kind != "last":
                    f_a(3)
                    f_b(3)
                if att:
                    y_a(2)
                    y_a(3)
                    t2_lo(0, 0)
                    t2_lo(0, 1)
                    y_b(2)
                    y_b(3)
                    y_c(2)
                    y_c(3)
                if kind == "last":
                    t2_lo(0, 2)
                    t2_lo(0, 3)
                    f_a(3)
                    f_b(3)

            bodies(dve, body)


_INS = ["L0_attn_hidden_states", "L0_attn_Wq", "L0_attn_bq", "L0_attn_Wv", "L0_attn_bv", "L0_attn_Wo", "L0_attn_bo",
        "L0_attn_latent_keys", "L0_ffn_W_up", "L0_ffn_W_gate", "L0_ffn_W_down"]


def kernel(**inputs):
    import numpy as _np
    import concourse.bacc as _bacc
    from concourse import mybir as _mybir
    from concourse.bass_utils import run_bass_kernel_spmd as _run

    nc = _bacc.Bacc("TRN2", target_bir_lowering=False, num_devices=1)
    arrays, args = {}, []
    for name in _INS:
        a = _np.ascontiguousarray(inputs[name])
        arrays[f"in_{name}"] = a
        args.append(nc.dram_tensor(f"in_{name}", a.shape, _mybir.dt.from_np(a.dtype), kind="ExternalInput").ap())
    shape = inputs["L0_attn_hidden_states"].shape
    o = nc.dram_tensor("out_dram", shape, _mybir.dt.float32, kind="ExternalOutput").ap()
    build(nc, *args, o)
    r = _run(nc, [arrays], core_ids=[0])
    return r.results[0]["out_dram"]
```

```python
from contextlib import ExitStack

import concourse.bass as bass
from concourse import mybir

ALU = mybir.AluOpType
ACT = mybir.ActivationFunctionType
AX = mybir.AxisListType
F32 = mybir.dt.float32
F16 = mybir.dt.float16
U32 = mybir.dt.uint32
RMAX = bass.bass_isa.ReduceOp.max
RADD = bass.bass_isa.ReduceOp.add

P = 128
D = 512
KD = D // P
H = 16
HD = D // H
NL = 64
TOPK = 4
E = 2048
NE = E // P
TT = 4
CH = TT * P
PADS = 8 - TOPK
LW = NL + PADS
EPS = 1e-5
QEPS = 1e-8

PAD = -3.0e38
HIT = -1.0e30
XS = 2.0 ** 11
WS = 2.0 ** 13
AS = 2.0 ** 5
PROJ = AS / (XS * WS)
PS = 2.0 ** 11
HS = 2.0 ** -26
TINY = 2.0 ** -100

LOGITS = (0, 2, 1, 3, 4, 5, 6, 7)


def pe_order(kind):
    att, ffn = kind != "tail", kind != "first"
    o = []
    if kind == "first":
        o += [("WT", 0, n) for n in range(KD)]
    if att:
        o += [("Q", 0, m) for m in range(KD)]
        o += [("L", 0, n) for n in LOGITS[:4]]
        if kind == "first":
            o += [("WT", 0, n) for n in range(KD, 3 * KD)]
        o += [("L", 0, n) for n in LOGITS[4:]]
    if ffn:
        o += [("DN", -1, 0), ("DN", -1, 1)]
    if att:
        o += [("VW", 0, m) for m in range(KD)]
    if kind == "last":
        return o + [("WO", 0, t) for t in range(TT)] + [("DN", -1, 2), ("DN", -1, 3)]
    if ffn:
        o += [("DN", -1, 2)]
    if att:
        o += [("WO", 0, 0), ("WO", 0, 1), ("WO", 0, 2)]
    if ffn:
        o += [("DN", -1, 3)]
    if att:
        o += [("WO", 0, 3)]
    return o


def ring_plan(kind):
    if kind == "first":
        seq = pe_order(kind)
        shift = -len(seq) % 4
        return {job: ((n + shift) % 4, seq[n - 4] if n >= 4 else None) for n, job in enumerate(seq)}
    if kind == "tail":
        before = [(w, c - 1, n) for w, c, n in pe_order("last")[-4:]]
    else:
        before = [("WO", -1, 1), ("WO", -1, 2), ("WO", -1, 3), ("WO", -1, 3)]
    seq = before + pe_order(kind)
    return {seq[n]: (n % 4, seq[n - 4]) for n in range(4, len(seq))}


def build(nc, x, Wq, bq, Wv, bv, Wo, bo, lat, Wu, Wg, Wd, out):
    NCH = x.shape[0] * x.shape[1] // CH
    with ExitStack() as ctx:
        def sb(name, shape, dt=F32):
            return ctx.enter_context(nc.sbuf_tensor(name, shape, dt))

        def sem(name):
            return ctx.enter_context(nc.semaphore(name))

        TU = sb("TU", [P, KD * E], F16)
        TG = sb("TG", [P, KD * E], F16)
        TD = sb("TD", [P, NE * D], F16)
        tu = TU[:, :].rearrange("p (k e) -> p k e", k=KD)
        tg = TG[:, :].rearrange("p (k e) -> p k e", k=KD)
        td = TD[:, :].rearrange("p (j d) -> p j d", j=NE)
        wT = [[sb(f"w{w}_{s}", [P, KD, D], F16) for s in ("hi", "lo")] for w in ("q", "v", "o")]
        latL = [sb(f"latL_{s}", [P, KD, 4 * NL], F16) for s in ("hi", "lo")]
        latV = [sb(f"latV_{s}", [P, H // 2, 2 * HD], F16) for s in ("hi", "lo")]
        bo_b = sb("bo_b", [P, D])
        id32 = sb("id32", [P, P])
        id16 = sb("id16", [P, P], F16)

        x_in = sb("x_in", [P, TT, D])
        x1 = sb("x1", [P, TT, D])
        XT = sb("XT", [P, 2, KD, CH], F16)
        qaT = [sb(f"qaT_{s}", [P, KD, CH], F16) for s in ("hi", "lo")]
        Lb = sb("Lb", [P, 2, H, LW])
        Lr = sb("Lr", [P, H, LW])
        PT = sb("PT", [P, 2, 8, CH], F16)
        X1T = sb("X1T", [P, 2, KD, CH], F16)
        hT = sb("hT", [P, 2, NE, CH], F16)
        ugt = sb("ugt", [P, 4, CH])
        p32 = sb("p32", [P, 2, CH])
        Pb = p32[:, :, :].rearrange("p a b -> p (a b)")
        row = sb("row", [P, 2, D])
        xn = sb("xn", [P, D])
        halves = sb("halves", [P, 2, 2 * D], F16)

        mv1 = sb("mv1", [P, TT, 2])
        st1 = sb("st1", [P, TT, 6])
        sty = sb("sty", [P, 2, 6])
        mvy = sb("mvy", [P, 2, 2])
        stx = sb("stx", [P, 2, 6])
        mvx = sb("mvx", [P, 2, 2])
        stf = sb("stf", [P, 2, 6])
        mvf = sb("mvf", [P, 2, 2])
        va1 = sb("va1", [P, TT])
        vay = sb("vay", [P, 2])
        vax = sb("vax", [P, 2])
        vaf = sb("vaf", [P, 2])
        rs1 = sb("rs1", [P, TT])
        rsy = sb("rsy", [P, 2])
        rsx = sb("rsx", [P, 2])
        rsf = sb("rsf", [P, 2])
        rcf = sb("rcf", [P, 2])
        nb1 = sb("nb1", [P, TT])
        nbx = sb("nbx", [P, 2])
        nby, nby_last = sb("nby", [P, TT]), sb("nby_last", [P, TT])
        nbf = sb("nbf", [P, 2])
        nh = sb("nh", [P, TT])
        v8 = sb("v8", [P, 2, H, 8])
        d4 = sb("d4", [P, 2, H, TOPK])
        s4 = sb("s4", [P, 2, H])
        r4 = sb("r4", [P, 2, H])
        bqc = sb("bqc", [P, KD])
        bvc = sb("bvc", [P, KD])
        bqs = sb("bqs", [P, KD])
        bvs = sb("bvs", [P, KD])
        mx = sb("mx", [P, 6])
        mg = sb("mg", [P, 4])
        ma = sb("ma", [P, 4])
        sc = sb("sc", [P, 4])
        inv = sb("inv", [P, 4])
        up = sb("upw", [P, 4])
        upb = sb("upb", [P, 2])
        clo = sb("clo", [P, 2])
        asum = sb("asum", [P, 24])
        tot = sb("tot", [P, 3])
        tota = sb("tota", [P, 3])
        sw = sb("sw", [P, 3])
        hw = sb("hw", [P, 3])
        nhw = sb("nhw", [P, 3])
        cu = sb("cu", [P, 1])
        cf = sb("cf", [P, 2])

        ug = ctx.enter_context(nc.psum_tensor("ug", [P, 4, CH], F32))
        ring = ctx.enter_context(nc.psum_tensor("ring", [P, 4, CH], F32))

        PER = {}

        def csem(name, n):
            PER[name] = n
            return sem(name)

        x_in_loaded = csem("x_in_loaded", 16)
        x_res_loaded = [sem(f"x_res_loaded{t}") for t in range(TT)]
        out_stored = [sem(f"out_stored{t}") for t in range(TT)]
        ln1_stats, ln1_mean, ln1_var, ln1_rstd, ln1_bias = (sem(f"ln1_{n}") for n in ("stats", "mean", "var", "rstd", "bias"))
        xn1_ready = sem("xn1_ready")
        x_hi, x_lo, x_t = sem("x_hi"), sem("x_lo"), [sem(f"x_t{s}") for s in range(2)]
        q_done, q32_ready, q_hi, q_lo = sem("q_done"), sem("q32_ready"), sem("q_hi"), sem("q_lo")
        q_lo3 = sem("q_lo3")
        l_done, l_ready = sem("l_done"), sem("l_ready")
        top8, v8_ready, d4_ready, e4_ready = sem("top8"), sem("v8_ready"), sem("d4_ready"), sem("e4_ready")
        sum_ready, recip_ready = sem("sum_ready"), sem("recip_ready")
        replaced, shifted, e_ready = sem("replaced"), sem("shifted"), sem("e_ready")
        p_raw, p_ready = sem("p_raw"), sem("p_ready")
        p_hi, p_lo, p_t = sem("p_hi"), sem("p_lo"), sem("p_t")
        vw_done, a32_ready, a_hi, a_lo = sem("vw_done"), sem("a32_ready"), sem("a_hi"), sem("a_lo")
        wo_done, y_ready = sem("wo_done"), sem("y_ready")
        y_stats, y_mean, y_var, y_rstd = (sem(f"y_{n}") for n in ("stats", "mean", "var", "rstd"))
        x1_ready = sem("x1_ready")
        ln2_stats, ln2_mean, ln2_var, ln2_rstd, ln2_bias = (sem(f"ln2_{n}") for n in ("stats", "mean", "var", "rstd", "bias"))
        xn2_ready = sem("xn2_ready")
        x1_hi, x1_lo, x1_t = sem("x1_hi"), sem("x1_lo"), [sem(f"x1_t{s}") for s in range(2)]
        ug_done, tanh_ready, t1_ready, h32_ready = sem("ug_done"), sem("tanh_ready"), sem("t1_ready"), sem("h32_ready")
        h_hi, h_lo = sem("h_hi"), sem("h_lo")
        dn_done = sem("dn_done")
        f_stats, f_mean, f_var, f_rstd, f_scale, f_bias, f_sum = (sem(f"f_{n}") for n in ("stats", "mean", "var", "rstd", "scale", "bias", "sum"))
        f_varc = sem("f_varc")
        out_ready = sem("out_ready")
        own_wait = sem("own_wait")
        own_wait_sp = sem("own_wait_sp")
        aw_loaded = [sem(f"aw_loaded{n}") for n in range(7)]
        w_loaded = [sem(f"w_loaded{n}") for n in range(24)]
        zeroed, id_zeroed, consts, idents = sem("zeroed"), sem("id_zeroed"), sem("consts"), sem("idents")
        mx_ready, mg_ready, ma_ready, sc_step, scales = (sem(n) for n in ("mx_ready", "mg_ready", "ma_ready", "sc_step", "scales"))
        wt_done, wt_hi, wt_lo = sem("wt_done"), sem("wt_hi"), sem("wt_lo")
        lat_done, lat_hi, lat_lo = sem("lat_done"), sem("lat_hi"), sem("lat_lo")
        asum_done, tot_ready, tota_ready, tern_step = (sem(n) for n in ("asum_done", "tot_ready", "tota_ready", "tern_step"))
        tern_scale = sem("tern_scale")
        sign_ready = sem("sign_ready")
        own_below, own_asum = sem("own_below"), sem("own_asum")
        below_ready, tern_ready, tp_done, tp_evicted = (sem(n) for n in ("below_ready", "tern_ready", "tp_done", "tp_evicted"))

        FREED = {"Q": (q32_ready, KD), "L": (l_ready, 8),
                 "DN": (f_sum, TT), "WT": (wt_lo, 3 * KD), "VW": (a32_ready, KD), "WO": (y_ready, TT)}

        def wait(eng, s, c, per, n):
            v = c * per + max(n, 0)
            if not isinstance(v, int) or v > 0:
                eng.wait_ge(s, v)

        hT32 = hT[:, :, :, :].rearrange("p s e t -> p (s e t)").bitcast(F32)
        td32 = TD[:, :].bitcast(F32)
        x1t32 = X1T[:, :, :, :].rearrange("p s k t -> p (s k t)").bitcast(F32)
        ugt32 = ugt[:, :, :].rearrange("p a b -> p (a b)")
        tg32 = TG[:, :].bitcast(F32)
        raw_a = [TU[:, :].bitcast(F32)[:, 0:2048], tg32[:, 0:2048], tg32[:, 2048:4096]]
        latr = row[:, 0, :]
        stage_hT = [hT32[:, 1024 * q:1024 * q + 1024] for q in range(8)]
        stage_mix = ([td32[:, 1024 * q:1024 * q + 1024] for q in range(4)]
                     + [x1t32[:, 1024 * q:1024 * q + 1024] for q in range(2)]
                     + [ugt32[:, 1024 * q:1024 * q + 1024] for q in range(2)])
        stages = [stage_hT, stage_mix, stage_hT]
        slots_a = [x1[:, s, :].bitcast(F16) for s in range(TT)]
        slots_d = [ugt[:, s, :].bitcast(F16) for s in range(4)]
        tern = [(slots_a if n < 16 else slots_d)[n % 4] for n in range(24)]
        ASUM_DVE = (0, 1, 2, 3)
        AHEAD = 3
        BELOW_DVE = (0, 1, 2, 3, 8, 16, 17, 18, 19, 20, 21, 22, 23)
        BELOW_ACT = (5, 7, 9, 11, 13, 15)
        tpb = [ug[:, s, :].bitcast(F16) for s in range(2)]
        junk = ug[:, 2:4, :].rearrange("p a b -> p (a b)")

        xv = x.rearrange("b (c p t) d -> (b c) p t d", p=P, t=TT)
        ov = out.rearrange("b (c p t) d -> (b c) p t d", p=P, t=TT)

        out_buf = [Lr[:, :, :].rearrange("p h l -> p (h l)")[:, D * s:D * s + D] for s in range(2)]

        def residual(is_last):
            return x_in if is_last else x1

        def split_buffers(kind, c, t):
            if kind == "first" and c == 0:
                return (qaT[t // 2][:, :, :].rearrange("p k t -> p (k t)").bitcast(F32)[:, (t % 2) * D:(t % 2 + 1) * D],
                        PT[:, 0, 2 * t:2 * t + 2, :].rearrange("p k t -> p (k t)"))
            if kind == "first" and c == 1:
                return xn[:, :], X1T[:, t // 2, 2 * (t % 2):2 * (t % 2) + 2, :].rearrange("p k t -> p (k t)")
            return xn[:, :], halves[:, t % 2, :]

        def slot_free(eng, n):
            if 16 <= n < 20:
                eng.wait_ge(tern_ready, 16)
            elif n >= 4:
                eng.wait_ge(tp_done, n - 3)

        def chunk(v, c):
            return v[c] if isinstance(c, int) else v[bass.ds(c, 1)].rearrange("a p t d -> (a p) t d")

        plans = {kind: ring_plan(kind) for kind in ("first", "mid", "last", "tail")}

        def bodies(eng, body):
            body(0, "first", True, False, True)
            with eng.Fori(1, NCH - 1) as i:
                body(i, "mid", True, True, True)
            body(NCH - 1, "last", True, True, False)
            body(NCH, "tail", False, True, False)

        WSCALE = (0, 2, 3)

        block = ctx.enter_context(nc.Block())

        @block.sync
        def _(sp):
            def load_ffn(w, W, *pieces):
                v = W.rearrange("(q r p) d -> q p r d", p=P, r=2)
                for q in pieces:
                    sp.dma_start(stages[w][q].rearrange("p (r d) -> p r d", r=2), v[q]).then_inc(w_loaded[8 * w + q], 16)

            def transpose_rows(dst, t, src, done):
                sp.dma_start_transpose(dst[:, :, :, t * P:(t + 1) * P].rearrange("p s k t -> p (s k) t"),
                                       src).then_inc(done[t % 2], 16)

            sp.dma_start(x_in[:, :, :], xv[0]).then_inc(x_in_loaded, 16)
            sp.dma_start(raw_a[0].rearrange("p (m d) -> p m d", m=KD), Wq.rearrange("(m p) d -> p m d", p=P)).then_inc(aw_loaded[0], 16)
            for s in range(2):
                sp.dma_start(latr[NL * s:NL * s + NL, :], lat).then_inc(aw_loaded[3], 16)
            sp.dma_start(bqc[:, :], bq.rearrange("(m p) -> p m", p=P), allow_slow_non_contiguous=True).then_inc(aw_loaded[4], 16)
            load_ffn(0, Wu, 0, 1, 2, 3)
            for t in range(TT):
                sp.wait_ge(x_lo, t + 1)
                transpose_rows(XT, t, split_buffers("first", 0, t)[1], x_t)
            load_ffn(0, Wu, 4, 5, 6, 7)
            sp.dma_start(bvc[:, :], bv.rearrange("(m p) -> p m", p=P), allow_slow_non_contiguous=True).then_inc(aw_loaded[5], 16)
            sp.dma_start(raw_a[1].rearrange("p (m d) -> p m d", m=KD), Wv.rearrange("(m p) d -> p m d", p=P)).then_inc(aw_loaded[1], 16)
            sp.dma_start(raw_a[2].rearrange("p (m d) -> p m d", m=KD), Wo.rearrange("(m p) d -> p m d", p=P)).then_inc(aw_loaded[2], 16)
            load_ffn(1, Wg, *range(8))
            sp.dma_start(bo_b[:, :], bo.rearrange("(a d) -> a d", a=1).broadcast_to([P, D])).then_inc(aw_loaded[6], 16)

            def body(i, kind, att, ffn, nxt):
                def s1(t):
                    wait(sp, x_lo, i + 1, TT, t + 1)
                    sp.sem_inc(own_wait_sp, 1)
                    wait(sp, vw_done, i, KD, KD)
                    sp.sem_inc(own_wait_sp, 1)
                    transpose_rows(XT, t, split_buffers(kind, 1, t)[1], x_t)

                def t2(c, t):
                    wait(sp, x1_lo, i + c, TT, t + 1)
                    sp.sem_inc(own_wait_sp, 1)
                    wait(sp, ug_done, i + c, NE, 0)
                    sp.sem_inc(own_wait_sp, 1)
                    if kind == "first" and t == 0:
                        for s in range(2):
                            sp.wait_ge(x_t[s], 64)
                    transpose_rows(X1T, t, halves[:, t % 2, :], x1_t)

                def pt(t):
                    wait(sp, p_lo, i, TT, t + 1)
                    sp.sem_inc(own_wait_sp, 1)
                    wait(sp, vw_done, i, KD, 0)
                    sp.sem_inc(own_wait_sp, 1)
                    sp.dma_start_transpose(PT[:, :, :, t * P:(t + 1) * P].rearrange("p s k t -> p (s k) t"),
                                           halves[:, :, :].rearrange("p s d -> p (s d)")).then_inc(p_t, 16)

                def out(t):
                    wait(sp, out_ready, i - 1, TT, t + 1)
                    sp.dma_start(chunk(ov, i - 1)[:, t, :], out_buf[t % 2]).then_inc(out_stored[t], 16)

                def reload(t):
                    wait(sp, f_sum, i - 1, TT, t + 1)
                    sp.dma_start(x1[:, t, :], chunk(xv, i)[:, t, :]).then_inc(x_res_loaded[t], 16)

                def down_piece(q):
                    sp.wait_ge(tern_ready, q + 1)
                    sp.dma_start(stages[2][q], Wd.rearrange("(a p) (b e) -> a b p e", p=P, b=2)[q // 2, q % 2]).then_inc(w_loaded[16 + q], 16)

                if ffn and att:
                    t2(-1, 2)
                    t2(-1, 3)
                if nxt:
                    wait(sp, xn1_ready, i, TT, TT)
                    sp.dma_start(x_in[:, :, :], chunk(xv, i + 1)).then_inc(x_in_loaded, 16)
                if kind == "first":
                    for q in range(8):
                        down_piece(q)
                    pt(0)
                    pt(1)
                    pt(2)
                    pt(3)
                    sp.wait_ge(tp_done, 16)
                    for t in range(TT):
                        sp.dma_start(x1[:, t, :], xv[0, :, t, :]).then_inc(x_res_loaded[t], 16)
                elif att:
                    for t in range(TT):
                        pt(t)
                if ffn:
                    for t in range(2):
                        if nxt:
                            reload(t)
                        out(t)
                if nxt:
                    for t in range(TT):
                        s1(t)
                if kind == "last":
                    for t in range(TT):
                        t2(0, t)
                if ffn and nxt:
                    reload(2)
                if ffn:
                    out(2)
                if nxt:
                    t2(0, 0)
                    t2(0, 1)
                if ffn and nxt:
                    reload(3)
                if ffn:
                    out(3)

            bodies(sp, body)
            for t in range(TT):
                sp.wait_ge(out_stored[t], 16 * NCH)

        @block.tensor
        def _(pe):
            def body(i, kind, att, ffn, nxt):
                plan = plans[kind]
                j = i - 1

                def bank_of(what, c, n):
                    bank, before = plan[(what, c, n)]
                    if before:
                        pk, pc, pn = before
                        s, per = FREED[pk]
                        if pk == "L":
                            pn = LOGITS.index(pn)
                        wait(pe, s, i + pc, per, pn + 1)
                    return bank

                def weights(w):
                    pe.wait_ge(aw_loaded[w], 16)
                    for m in range(KD):
                        bank = bank_of("WT", 0, KD * w + m)
                        for k in range(KD):
                            last = pe.transpose(ring[:, bank, k * P:(k + 1) * P],
                                                raw_a[w][:, m * D + k * P:m * D + (k + 1) * P], id32[:, :])
                        last.then_inc(wt_done, 1)

                def latents():
                    pe.wait_ge(aw_loaded[3], 32)
                    for g in range(KD):
                        last = pe.transpose(ug[:, 0, g * NL:(g + 1) * NL], latr[0:NL, g * P:(g + 1) * P],
                                            id32[0:NL, 0:NL])
                    last.then_inc(lat_done, 1)

                def ternary(n):
                    if n == 0:
                        pe.wait_ge(idents, 2)
                        pe.wait_ge(lat_lo, 1)
                    pe.wait_ge(tern_ready, n + 1)
                    if n >= 2:
                        pe.wait_ge(tp_evicted, n - 1)
                    for b in range(8):
                        o = ((b % 4) * 2 + b // 4) if n < 16 else b
                        last = pe.transpose(tpb[n % 2][:, o * P:(o + 1) * P], tern[n][:, b * P:(b + 1) * P], id16[:, :])
                    last.then_inc(tp_done, 1)

                def project(w, bank, m, stop):
                    n = 0
                    for k in range(KD):
                        for a, b in ((0, 0), (0, 1), (1, 0)):
                            n += 1
                            last = pe.matmul(ring[:, bank, :], wT[w][a][:, k, m * P:(m + 1) * P], XT[:, b, k, :],
                                             start=(n == 1), stop=(stop and n == 3 * KD), skip_group_check=not stop)
                    return last

                def q(m):
                    bank = bank_of("Q", 0, m)
                    if m == 0:
                        for s in range(2):
                            wait(pe, x_t[s], i, 32, 32)
                        if kind == "first":
                            pe.wait_ge(wt_lo, KD)
                    project(0, bank, m, True).then_inc(q_done, 1)

                def logits(*tiles):
                    for b, t in [(b, t) for b in range(2) for t in tiles]:
                        bank = bank_of("L", 0, 2 * t + b)
                        if t == 0:
                            wait(pe, q_lo, i, KD - 1, b + 2)
                            if b:
                                wait(pe, q_lo3, i, 1, 1)
                            if kind == "first" and b == 0:
                                pe.wait_ge(lat_lo, 1)
                        for g in (2 * b, 2 * b + 1):
                            for n, (a, c) in enumerate(((0, 0), (0, 1), (1, 0))):
                                last = pe.matmul(ring[:, bank, (g % 2) * 256:(g % 2) * 256 + 256],
                                                 qaT[a][:, g, t * P:(t + 1) * P], latL[c][:, g, :],
                                                 start=(n == 0), stop=(n == 2))
                        last.then_inc(l_done, 1)

                def vw(m):
                    bank = bank_of("VW", 0, m)
                    if m == 0 and kind == "first":
                        pe.wait_ge(wt_lo, 3 * KD)
                    project(1, bank, m, False)
                    if m == 0:
                        wait(pe, p_t, i, 16 * TT, 16 * TT)
                        if kind == "first":
                            pe.wait_ge(lat_lo, 2)
                    for n, (a, c) in enumerate(((0, 0), (0, 1), (1, 0))):
                        for s in range(2):
                            last = pe.matmul(ring[64 * s:64 * s + 64, bank, :], latV[a][:, 2 * m + s, :],
                                             PT[:, c, 2 * m + s, :], start=False, stop=(n == 2), skip_group_check=True)
                    last.then_inc(vw_done, 1)

                def wo(t):
                    bank = bank_of("WO", 0, t)
                    n = 0
                    for k in range(KD):
                        if t == 0:
                            wait(pe, a_lo, i, KD, k + 1)
                        for a, b in ((0, 0), (0, 1), (1, 0)):
                            n += 1
                            last = pe.matmul(ring[:, bank, :], qaT[a][:, k, t * P:(t + 1) * P], wT[2][b][:, k, :],
                                             start=(n == 1), stop=(n == 3 * KD))
                    last.then_inc(wo_done, 1)

                def upgate(e):
                    if e == 0:
                        for s in range(2):
                            wait(pe, x1_t[s], j, 32, 32)
                    wait(pe, h32_ready, j, NE, e - 1)
                    for s, w in ((0, tu), (1, tg)):
                        for k in range(KD):
                            for b in range(2):
                                last = pe.matmul(ug[:, 2 * (e % 2) + s, :], w[:, k, e * P:(e + 1) * P], X1T[:, b, k, :],
                                                 start=(k == 0 and b == 0), stop=(k == KD - 1 and b == 1))
                    last.then_inc(ug_done, 1)

                def down(t):
                    bank = bank_of("DN", -1, t)
                    for e in range(NE):
                        if t == 0:
                            wait(pe, h_lo, j, NE, e + 1)
                        for a in range(2):
                            last = pe.matmul(ring[:, bank, :], hT[:, a, e, t * P:(t + 1) * P], td[:, e, :],
                                             start=(e == 0 and a == 0), stop=(e == NE - 1 and a == 1))
                    last.then_inc(dn_done, 1)

                if kind == "first":
                    pe.wait_ge(idents, 1)
                    weights(0)
                    latents()
                if att:
                    for m in range(KD):
                        q(m)
                if kind == "first":
                    ternary(0)
                    ternary(1)
                if att:
                    logits(0, 1)
                if kind == "first":
                    weights(1)
                    after = {3: [(weights, 2)], 5: [(logits, 2)], 8: [(logits, 3)], 15: [(vw, 0)],
                             17: [(vw, 1)], 19: [(vw, 2)], 21: [(vw, 3)],
                             23: [(wo, 0), (wo, 1), (wo, 2), (wo, 3)]}
                    for n in range(24):
                        if n >= 2:
                            ternary(n)
                        for f, *a in after.get(n, ()):
                            f(*a)
                    return
                for e in range(NE):
                    upgate(e)
                    if att and e == 5:
                        logits(2)
                    if att and e == 9:
                        logits(3)
                down(0)
                down(1)
                if att:
                    for m in range(KD):
                        vw(m)
                if kind == "last":
                    for t in range(TT):
                        wo(t)
                down(2)
                if nxt:
                    wo(0)
                    wo(1)
                    wo(2)
                down(3)
                if nxt:
                    wo(3)

            bodies(pe, body)

        @block.scalar
        def _(act):
            def body(i, kind, att, ffn, nxt):
                plan = plans[kind]
                j = i - 1

                def blocks(what, c, n):
                    return ring[:, plan[(what, c, n)][0], :].rearrange("p (k b) -> p k b", k=KD)

                def s1_rows(c, t):
                    wait(act, ln1_bias, i + c, 1, 1)
                    if kind == "first" and c == 0:
                        pass
                    elif t:
                        wait(act, x_lo, i + c, TT, t)
                    elif kind != "first":
                        wait(act, x1_lo, i - 1, TT, TT)
                    rows, half = split_buffers(kind, c, t)
                    act.activation(rows, x_in[:, t, :], ACT.Identity, scale=rs1[:, t:t + 1],
                                   bias=nb1[:, t:t + 1]).then_inc(xn1_ready, 1)
                    wait(act, xn1_ready, i + c, TT, t + 1)
                    if kind == "first":
                        if c == 1 and t == 0:
                            act.wait_ge(tern_ready, 14)
                    elif t < 2:
                        wait(act, p_t, i + c, 16 * TT, 0)
                    else:
                        wait(act, x_t[t % 2], i + c, 32, 16)
                    act.activation(half[:, 0:D], rows, ACT.Copy).then_inc(x_hi, 1)

                def t2_rows(c, t):
                    wait(act, ln2_bias, i + c, TT, t + 1)
                    if t:
                        wait(act, x1_lo, i + c, TT, t)
                    elif nxt:
                        wait(act, x_lo, i + 1, TT, TT)
                    else:
                        wait(act, x1_lo, i - 1, TT, TT)
                    act.activation(xn[:, :], residual(kind == "last" and c == 0)[:, t, :], ACT.Identity, scale=rsx[:, t % 2:t % 2 + 1],
                                   bias=nbx[:, t % 2:t % 2 + 1]).then_inc(xn2_ready, 1)
                    wait(act, xn2_ready, i + c, TT, t + 1)
                    if t >= 2:
                        wait(act, x1_t[t % 2], i + c, 32, 16)
                    elif kind == "mid":
                        wait(act, x_t[t % 2], i + 1, 32, 32)
                    else:
                        wait(act, p_t, i, 16 * TT, 16 * TT)
                    act.activation(halves[:, t % 2, 0:D], xn[:, :], ACT.Copy).then_inc(x1_hi, 1)

                def weights_hi(w):
                    if w < 2:
                        act.wait_ge(scales, w + 1)
                    for m in range(KD):
                        act.wait_ge(wt_done, KD * w + m + 1)
                        act.activation(wT[w][0][:, :, m * P:(m + 1) * P], blocks("WT", 0, KD * w + m), ACT.Copy,
                                       scale=up[:, WSCALE[w]:WSCALE[w] + 1]).then_inc(wt_hi, 1)

                def latL_hi():
                    act.wait_ge(lat_done, 1)
                    act.wait_ge(zeroed, 1)
                    for hh in range(4):
                        rows = slice(HD * hh, HD * hh + HD)
                        last = act.activation(latL[0][rows, :, hh * NL:(hh + 1) * NL],
                                              ug[rows, 0, 0:KD * NL].rearrange("p (g l) -> p g l", g=KD), ACT.Copy,
                                              scale=up[rows, 1:2])
                    last.then_inc(lat_hi, 1)

                def latV_hi():
                    for hh in range(2):
                        rows = slice(NL * hh, NL * hh + NL)
                        last = act.activation(latV[0][rows, :, hh * HD:(hh + 1) * HD],
                                              latr[rows, :].rearrange("p (j h d) -> p j h d", h=2, d=HD)[:, :, hh, :],
                                              ACT.Copy, scale=up[rows, 2:3])
                    last.then_inc(lat_hi, 1)

                def abs_sum(*pieces):
                    for n in pieces:
                        act.wait_ge(w_loaded[n], 16)
                        before = n - len(ASUM_DVE)
                        if before:
                            act.wait_ge(asum_done, before)
                        act.activation(junk, stages[n // 8][n % 8], ACT.Abs, accum_out=asum[:, n:n + 1]).then_inc(asum_done, 1)

                def sign(n):
                    w, q = n // 8, n % 8
                    act.wait_ge(tern_scale, w + 1)
                    slot_free(act, n)
                    act.activation(tern[n], stages[w][q], ACT.Sign, bias=hw[:, w:w + 1]).then_inc(sign_ready, 1)

                def evict_ternary(n):
                    act.wait_ge(tp_done, n + 1)
                    w, q = n // 8, n % 8
                    if w < 2:
                        dst = (tu, tg)[w][:, :, 256 * q:256 * q + 256]
                        src = tpb[n % 2].rearrange("p (k e) -> p k e", k=KD)
                    else:
                        dst = td[:, 8 * (q % 2):8 * (q % 2) + 8, (q // 2) * P:(q // 2 + 1) * P]
                        src = tpb[n % 2].rearrange("p (j d) -> p j d", j=8)
                    act.activation(dst, src, ACT.Copy).then_inc(tp_evicted, 1)

                def q(m):
                    wait(act, q_done, i, KD, m + 1)
                    if m < 2:
                        wait(act, a_lo, i - 1, KD, m + 3)
                    else:
                        wait(act, q_lo, i, KD - 1, m - 1)
                    act.activation(p32[:, m % 2, :], ring[:, plan[("Q", 0, m)][0], :], ACT.Identity,
                                   scale=PROJ, bias=bqs[:, m:m + 1]).then_inc(q32_ready, 1)
                    wait(act, q32_ready, i, KD, m + 1)
                    wait(act, wo_done, i, TT, 0)
                    act.activation(qaT[0][:, m, :], p32[:, m % 2, :], ACT.Copy).then_inc(q_hi, 1)

                def logits(*tiles):
                    for b, t in [(b, t) for b in range(2) for t in tiles]:
                        wait(act, l_done, i, 8, LOGITS.index(2 * t + b) + 1)
                        if b == 0:
                            wait(act, p_ready, i, TT, t - 1)
                        act.activation(Lb[:, t % 2, 8 * b:8 * b + 8, 0:NL],
                                       ring[:, plan[("L", 0, 2 * t + b)][0], :].rearrange("p (h l) -> p h l", h=8),
                                       ACT.Copy, scale=clo[:, 0:1]).then_inc(l_ready, 1)

                def exp4(t):
                    wait(act, d4_ready, i, TT, t + 1)
                    act.activation(d4[:, t % 2, :, :], d4[:, t % 2, :, :], ACT.Exp).then_inc(e4_ready, 1)

                def exps(t):
                    wait(act, shifted, i, TT, t + 1)
                    act.activation(Lb[:, t % 2, :, 0:NL], Lb[:, t % 2, :, 0:NL], ACT.Exp).then_inc(e_ready, 1)

                def probs_hi(t):
                    wait(act, p_ready, i, TT, t + 1)
                    if t:
                        wait(act, p_t, i, 16 * TT, 16 * t)
                    for s in range(2):
                        if t == 0 and ffn:
                            wait(act, x1_t[s], i - 1, 32, 32)
                    act.activation(halves[:, 0, :], Pb, ACT.Copy, scale=PS).then_inc(p_hi, 1)

                def vw(m):
                    wait(act, vw_done, i, KD, m + 1)
                    if m == 0:
                        wait(act, q_lo, i, KD - 1, KD - 1)
                    elif m == 1:
                        wait(act, q_lo3, i, 1, 1)
                    else:
                        wait(act, a_lo, i, KD, m - 1)
                    act.activation(p32[:, m % 2, :], ring[:, plan[("VW", 0, m)][0], :], ACT.Identity,
                                   scale=PROJ, bias=bvs[:, m:m + 1]).then_inc(a32_ready, 1)
                    wait(act, a32_ready, i, KD, m + 1)
                    wait(act, l_done, i, 8, 8)
                    act.activation(qaT[0][:, m, :], p32[:, m % 2, :], ACT.Copy).then_inc(a_hi, 1)

                def tanh(e):
                    wait(act, ug_done, j, NE, e + 1)
                    wait(act, h32_ready, j, NE, e - 1)
                    act.activation(ugt[:, e % 2, :], ug[:, 2 * (e % 2), :], ACT.Tanh, scale=cu[:, 0:1]).then_inc(tanh_ready, 1)

                def hidden_hi(e):
                    wait(act, h32_ready, j, NE, e + 1)
                    if e == 0:
                        wait(act, dn_done, j, TT, 0)
                    act.activation(hT[:, 0, e, :], ugt[:, 2 + e % 2, :], ACT.Copy).then_inc(h_hi, 1)

                def out_rows(t):
                    wait(act, f_sum, j, TT, t + 1)
                    act.activation(out_buf[t % 2], out_buf[t % 2], ACT.Identity, bias=nbf[:, t % 2:t % 2 + 1]).then_inc(out_ready, 1)

                if kind == "first":
                    for t in range(TT):
                        s1_rows(0, t)
                    weights_hi(0)
                    latL_hi()
                    abs_sum(4, 5, 6, 7)
                if att:
                    for m in range(KD):
                        q(m)
                        if ffn and m == 0:
                            t2_rows(-1, 2)
                        if ffn and m == 1:
                            t2_rows(-1, 3)
                if att:
                    logits(0, 1)
                if kind == "first":
                    evict_ternary(0)
                    evict_ternary(1)
                    weights_hi(1)
                    after = {0: [(exp4, 0), (abs_sum, 8)], 1: [(exps, 0), (abs_sum, 9, 10)], 2: [(abs_sum, 11, 12)],
                             3: [(abs_sum, 13, 14)], 4: [(abs_sum, 15), (weights_hi, 2), (latV_hi,)], 5: [(probs_hi, 0), (exp4, 1)], 6: [(logits, 2), (exps, 1)],
                             7: [(abs_sum, 16, 17)], 8: [(exp4, 2), (abs_sum, 18, 19)], 9: [(probs_hi, 1), (logits, 3), (exps, 2), (abs_sum, 20)],
                             10: [(abs_sum, 21, 22)], 11: [(exp4, 3), (abs_sum, 23)], 12: [(probs_hi, 2), (exps, 3)],
                             13: [(probs_hi, 3)], 16: [(vw, 0)], 17: [(s1_rows, 1, 0)], 18: [(vw, 1)], 19: [(s1_rows, 1, 1)],
                             20: [(vw, 2)], 21: [(s1_rows, 1, 2)],
                             22: [(vw, 3)], 23: [(s1_rows, 1, 3)], 24: [(t2_rows, 0, 0), (t2_rows, 0, 1)]}
                    for n in range(25):
                        if n > 2:
                            evict_ternary(n - 1)
                        if n + 1 + AHEAD in BELOW_ACT:
                            sign(n + 1 + AHEAD)
                        for f, *a in after.get(n, ()):
                            f(*a)
                    return
                for e in range(NE):
                    if ffn:
                        tanh(e)
                        if e:
                            hidden_hi(e - 1)
                    if not att:
                        continue
                    if e in (2, 4, 8, 12):
                        exp4((2, 4, 8, 12).index(e))
                    if e in (3, 6, 10, 14):
                        exps((3, 6, 10, 14).index(e))
                    if e == 5:
                        probs_hi(0)
                        logits(2)
                    if e == 9:
                        probs_hi(1)
                        logits(3)
                    if e == 13:
                        probs_hi(2)
                if ffn:
                    hidden_hi(NE - 1)
                if att:
                    probs_hi(3)
                if ffn:
                    out_rows(0)
                if nxt:
                    s1_rows(1, 0)
                    s1_rows(1, 1)
                if ffn:
                    out_rows(1)
                if att:
                    for m in range(KD):
                        vw(m)
                if nxt:
                    s1_rows(1, 2)
                    s1_rows(1, 3)
                if kind == "last":
                    for t in range(TT):
                        t2_rows(0, t)
                if ffn:
                    out_rows(2)
                if nxt:
                    t2_rows(0, 0)
                    t2_rows(0, 1)
                if ffn:
                    out_rows(3)

            bodies(act, body)

        @block.gpsimd
        def _(pool):
            pool.memset(id32[:, :], 0.0).then_inc(id_zeroed, 1)
            pool.memset(nh[:, :], -0.5).then_inc(consts, 1)
            pool.wait_ge(id_zeroed, 1)
            pool.affine_select(out=id32[:, :], in_=id32[:, :], compare_op=ALU.not_equal, fill=1.0, base=0,
                               pattern=[[-1, P]], channel_multiplier=1).then_inc(idents, 1)
            for s in range(2):
                pool.memset(latV[s][:, :, :], 0.0)
                pool.memset(latL[s][:, :, :], 0.0)
            pool.memset(Lb[:, :, :, NL:LW], PAD).then_inc(zeroed, 1)
            pool.wait_ge(consts, 1)

            def rstd(dst, src, width, var_ready, c, per, n, done):
                wait(pool, var_ready, c, per, n)
                pool.tensor_tensor(dst, src, nh[:, 0:width], ALU.pow).then_inc(done, 1)

            def ln1_rstd_of(c):
                rstd(rs1[:, :], va1[:, :], TT, ln1_var, c, 1, 1, ln1_rstd)

            ln1_rstd_of(0)

            def all_maxima(g):
                pool.wait_ge(mg_ready, g + 1)
                pool.partition_all_reduce(ma[:, 2 * g:2 * g + 2], mg[:, 2 * g:2 * g + 2], P, RMAX).then_inc(ma_ready, 1)

            all_maxima(0)

            def all_sum(w):
                pool.wait_ge(tot_ready, w + 1)
                pool.partition_all_reduce(tota[:, w:w + 1], tot[:, w:w + 1], P, RADD).then_inc(tota_ready, 1)

            def below(n):
                w, q = n // 8, n % 8
                if n in BELOW_DVE or n in BELOW_ACT:
                    return
                pool.wait_ge(tern_scale, w + 1)
                slot_free(pool, n)
                pool.tensor_scalar(tern[n], stages[w][q], nhw[:, w:w + 1], None, ALU.is_lt).then_inc(below_ready, 1)

            def body(i, kind, att, ffn, nxt):
                j = i - 1

                def low_q(m):
                    wait(pool, q_hi, i, KD, m + 1)
                    pool.tensor_tensor(qaT[1][:, m, :], p32[:, m % 2, :], qaT[0][:, m, :], ALU.subtract).then_inc(q_lo, 1)

                def low_a(m):
                    wait(pool, a_hi, i, KD, m + 1)
                    pool.tensor_tensor(qaT[1][:, m, :], p32[:, m % 2, :], qaT[0][:, m, :], ALU.subtract).then_inc(a_lo, 1)

                def shift(t):
                    wait(pool, replaced, i, TT, t + 1)
                    buf = Lb[:, t % 2, :, 0:NL]
                    pool.tensor_tensor(buf, buf, v8[:, t % 2, :, 0:1].broadcast_to([P, H, NL]), ALU.subtract).then_inc(shifted, 1)

                def normalise(t):
                    wait(pool, recip_ready, i, TT, t + 1)
                    wait(pool, p_raw, i, TT, t + 1)
                    wait(pool, p_lo, i, TT, t)
                    pool.tensor_tensor(Pb.rearrange("p (h l) -> p h l", h=H), Lb[:, t % 2, :, 0:NL],
                                       r4[:, t % 2, :].rearrange("p (h a) -> p h a", a=1).broadcast_to([P, H, NL]),
                                       ALU.mult).then_inc(p_ready, 1)

                def hidden_lo(e):
                    wait(pool, h_hi, j, NE, e + 1)
                    pool.tensor_tensor(hT[:, 1, e, :], ugt[:, 2 + e % 2, :], hT[:, 0, e, :], ALU.subtract).then_inc(h_lo, 1)

                def rstd_y(t):
                    rstd(rsy[:, t % 2:t % 2 + 1], vay[:, t % 2:t % 2 + 1], 1, y_var, i, TT, t + 1, y_rstd)

                def rstd_x(c, t):
                    rstd(rsx[:, t % 2:t % 2 + 1], vax[:, t % 2:t % 2 + 1], 1, ln2_var, i + c, TT, t + 1, ln2_rstd)

                def rstd_f(t):
                    rstd(rsf[:, t % 2:t % 2 + 1], vaf[:, t % 2:t % 2 + 1], 1, f_var, j, TT, t + 1, f_rstd)

                if kind == "first":
                    all_sum(0)
                if att:
                    for m in range(KD):
                        if m < 3:
                            low_q(m)
                        if ffn and m == 0:
                            rstd_x(-1, 3)
                        if kind == "first" and m == 2:
                            all_maxima(1)
                if kind == "first":
                    after = {0: [(shift, 0)], 3: [(normalise, 0)], 5: [(all_sum, 1), (shift, 1)], 7: [(normalise, 1)],
                             8: [(shift, 2)], 10: [(normalise, 2)], 12: [(shift, 3), (normalise, 3), (all_sum, 2), (ln1_rstd_of, i + 1)],
                             23: [(low_a, 0), (low_a, 1), (low_a, 2), (low_a, 3), (rstd_y, 0), (rstd_y, 1),
                                  (rstd_x, 0, 0), (rstd_x, 0, 1), (rstd_y, 2), (rstd_y, 3), (rstd_x, 0, 2)]}
                    for n in range(24):
                        if n + 1 + AHEAD < 24:
                            below(n + 1 + AHEAD)
                        for f, *a in after.get(n, ()):
                            f(*a)
                    return
                for e in range(NE):
                    if ffn:
                        hidden_lo(e)
                    if not att:
                        continue
                    if e in (1, 4, 8, 12):
                        shift((1, 4, 8, 12).index(e))
                    if e in (2, 6, 10, 14):
                        normalise((2, 6, 10, 14).index(e))
                if nxt:
                    ln1_rstd_of(i + 1)
                if ffn:
                    rstd_f(0)
                    rstd_f(1)
                if att:
                    for m in range(KD):
                        low_a(m)
                if nxt:
                    rstd_f(2)
                if att:
                    rstd_y(0)
                    rstd_y(1)
                    rstd_x(0, 0)
                    rstd_x(0, 1)
                    rstd_y(2)
                if nxt:
                    rstd_f(3)
                    rstd_x(0, 2)
                    rstd_y(3)
                if kind == "last":
                    rstd_y(3)
                    rstd_x(0, 2)
                    rstd_x(0, 3)
                if not nxt:
                    rstd_f(2)
                    rstd_f(3)

            bodies(pool, body)

        @block.vector
        def _(dve):
            def maxima(src, s, v, col):
                dve.wait_ge(aw_loaded[s], v)
                dve.tensor_reduce(mx[:, col:col + 1], src, AX.X, ALU.max, apply_absolute_value=True).then_inc(mx_ready, 1)

            def powers(g):
                cols, one = slice(2 * g, 2 * g + 2), slice(g, g + 1)
                at = 6 * g
                dve.wait_ge(ma_ready, g + 1)
                dve.tensor_scalar(sc[:, cols], ma[:, cols], TINY, None, ALU.max).then_inc(sc_step, 1)
                dve.wait_ge(sc_step, at + 1)
                dve.tensor_scalar(sc[:, cols].bitcast(U32), sc[:, cols].bitcast(U32), 0x7F800000, None,
                                  ALU.bitwise_and).then_inc(sc_step, 1)
                dve.wait_ge(sc_step, at + 2)
                dve.reciprocal(inv[:, cols], sc[:, cols]).then_inc(sc_step, 1)
                dve.tensor_tensor(clo[:, one], sc[:, 2 * g:2 * g + 1], sc[:, 2 * g + 1:2 * g + 2], ALU.mult).then_inc(sc_step, 1)
                dve.wait_ge(sc_step, at + 4)
                dve.tensor_scalar(up[:, cols], inv[:, cols], WS, None, ALU.mult)
                dve.tensor_scalar(upb[:, one], inv[:, 2 * g:2 * g + 1], AS, None, ALU.mult).then_inc(sc_step, 1)
                dve.tensor_scalar(clo[:, one], clo[:, one], (float(HD) ** -0.5, 1.0)[g] / (AS * WS), None, ALU.mult).then_inc(sc_step, 1)
                dve.wait_ge(sc_step, at + 6)
                dve.tensor_scalar((bqs, bvs)[g][:, :], (bqc, bvc)[g][:, :], upb[:, one], None, ALU.mult).then_inc(scales, 1)

            def abs_sum(n):
                dve.wait_ge(w_loaded[n], 16)
                dve.tensor_reduce(asum[:, n:n + 1], stages[n // 8][n % 8], AX.X, ALU.add, apply_absolute_value=True).then_inc(own_asum, 1)

            def tern_total(w):
                dve.wait_ge(asum_done, 8 * w + 8 - len(ASUM_DVE))
                dve.wait_ge(own_asum, len(ASUM_DVE))
                dve.reduce_sum(tot[:, w:w + 1], asum[:, 8 * w:8 * w + 8], AX.X).then_inc(tot_ready, 1)

            def tern_scale_of(w):
                dve.wait_ge(tota_ready, w + 1)
                dve.tensor_scalar(sw[:, w:w + 1], tota[:, w:w + 1], 1.0 / (E * D), QEPS, ALU.mult, ALU.add).then_inc(tern_step, 1)
                dve.wait_ge(tern_step, w + 1)
                dve.tensor_scalar(hw[:, w:w + 1], sw[:, w:w + 1], 0.5, None, ALU.mult)
                dve.tensor_scalar(nhw[:, w:w + 1], sw[:, w:w + 1], -0.5, None, ALU.mult).then_inc(tern_scale, 1)
                dve.wait_ge(tern_scale, w + 1)

            def ternarise(n):
                w, q = n // 8, n % 8
                if n in BELOW_DVE:
                    slot_free(dve, n)
                    dve.tensor_scalar(tern[n], stages[w][q], nhw[:, w:w + 1], None, ALU.is_lt).then_inc(own_below, 1)
                    dve.wait_ge(own_below, BELOW_DVE.index(n) + 1)
                elif n in BELOW_ACT:
                    dve.wait_ge(sign_ready, BELOW_ACT.index(n) + 1)
                else:
                    dve.wait_ge(below_ready, n + 1 - sum(m < n for m in BELOW_DVE + BELOW_ACT))
                dve.scalar_tensor_tensor(out=tern[n], in0=stages[w][q], scalar=hw[:, w:w + 1], in1=tern[n],
                                         op0=ALU.is_gt, op1=ALU.min if n in BELOW_ACT else ALU.subtract).then_inc(tern_ready, 1)

            def ffn_scales():
                dve.tensor_scalar(cu[:, :], sw[:, 0:1], 0.5 / XS, None, ALU.mult)
                dve.tensor_tensor(cf[:, 0:1], sw[:, 0:1], sw[:, 1:2], ALU.mult).then_inc(tern_step, 1)
                dve.wait_ge(tern_step, 4)
                dve.scalar_tensor_tensor(out=cf[:, 1:2], in0=cf[:, 0:1], scalar=0.5 / (XS * XS * HS), in1=sw[:, 2:3],
                                         op0=ALU.mult, op1=ALU.mult).then_inc(tern_step, 1)
                dve.wait_ge(tern_step, 5)

            def body(i, kind, att, ffn, nxt):
                plan = plans[kind]
                j = i - 1

                def blocks(what, c, n):
                    return ring[:, plan[(what, c, n)][0], :].rearrange("p (k b) -> p k b", k=KD)

                def ln1_stat(c):
                    wait(dve, x_in_loaded, i + c, 16, 16)
                    for t in range(TT):
                        last = dve.bn_stats(st1[:, t, :], x_in[:, t, :])
                    last.then_inc(ln1_stats, 1)
                    wait(dve, ln1_stats, i + c, 1, 1)
                    dve.sem_inc(own_wait, 1)
                    for t in range(TT):
                        last = dve.bn_aggr(mv1[:, t, :], st1[:, t, :])
                    last.then_inc(ln1_mean, 1)
                    wait(dve, ln1_mean, i + c, 1, 1)
                    dve.tensor_scalar(va1[:, :], mv1[:, :, 1], XS ** -2, EPS * XS ** -2, ALU.mult, ALU.add).then_inc(ln1_var, 1)

                def ln1_biases(c):
                    wait(dve, ln1_rstd, i + c, 1, 1)
                    dve.scalar_tensor_tensor(out=nb1[:, :], in0=mv1[:, :, 0], scalar=-1.0, in1=rs1[:, :],
                                             op0=ALU.mult, op1=ALU.mult).then_inc(ln1_bias, 1)

                def s1_lo(c, t):
                    wait(dve, x_hi, i + c, TT, t + 1)
                    rows, half = split_buffers(kind, c, t)
                    dve.tensor_tensor(half[:, D:2 * D], rows, half[:, 0:D], ALU.subtract).then_inc(x_lo, 1)

                def weights_lo(w):
                    for m in range(KD):
                        dve.wait_ge(wt_hi, KD * w + m + 1)
                        dve.scalar_tensor_tensor(out=wT[w][1][:, :, m * P:(m + 1) * P], in0=blocks("WT", 0, KD * w + m),
                                                 scalar=up[:, WSCALE[w]:WSCALE[w] + 1],
                                                 in1=wT[w][0][:, :, m * P:(m + 1) * P],
                                                 op0=ALU.mult, op1=ALU.subtract).then_inc(wt_lo, 1)

                def low_q():
                    wait(dve, q_hi, i, KD, KD)
                    dve.tensor_tensor(qaT[1][:, 3, :], p32[:, 1, :], qaT[0][:, 3, :], ALU.subtract).then_inc(q_lo3, 1)

                def latL_lo():
                    dve.wait_ge(lat_hi, 1)
                    for hh in range(4):
                        rows = slice(HD * hh, HD * hh + HD)
                        last = dve.scalar_tensor_tensor(out=latL[1][rows, :, hh * NL:(hh + 1) * NL],
                                                        in0=ug[rows, 0, 0:KD * NL].rearrange("p (g l) -> p g l", g=KD),
                                                        scalar=up[rows, 1:2], in1=latL[0][rows, :, hh * NL:(hh + 1) * NL],
                                                        op0=ALU.mult, op1=ALU.subtract)
                    last.then_inc(lat_lo, 1)

                def latV_lo():
                    dve.wait_ge(lat_hi, 2)
                    for hh in range(2):
                        rows = slice(NL * hh, NL * hh + NL)
                        last = dve.scalar_tensor_tensor(out=latV[1][rows, :, hh * HD:(hh + 1) * HD],
                                                        in0=latr[rows, :].rearrange("p (j h d) -> p j h d", h=2, d=HD)[:, :, hh, :],
                                                        scalar=up[rows, 2:3], in1=latV[0][rows, :, hh * HD:(hh + 1) * HD],
                                                        op0=ALU.mult, op1=ALU.subtract)
                    last.then_inc(lat_lo, 1)

                def t2_lo(c, t):
                    wait(dve, x1_hi, i + c, TT, t + 1)
                    dve.tensor_tensor(halves[:, t % 2, D:2 * D], xn[:, :], halves[:, t % 2, 0:D], ALU.subtract).then_inc(x1_lo, 1)

                def hidden(e):
                    wait(dve, tanh_ready, j, NE, e + 1)
                    dve.scalar_tensor_tensor(out=ugt[:, e % 2, :], in0=ugt[:, e % 2, :], scalar=1.0,
                                             in1=ug[:, 2 * (e % 2), :], op0=ALU.add, op1=ALU.mult).then_inc(t1_ready, 1)
                    wait(dve, t1_ready, j, NE, e + 1)
                    wait(dve, h_lo, j, NE, e - 1)
                    dve.scalar_tensor_tensor(out=ugt[:, 2 + e % 2, :], in0=ugt[:, e % 2, :], scalar=HS,
                                             in1=ug[:, 2 * (e % 2) + 1, :], op0=ALU.mult, op1=ALU.mult).then_inc(h32_ready, 1)

                def maxes(t, b):
                    wait(dve, l_ready, i, 8, LOGITS.index(2 * t + b) + 1)
                    if b == 0:
                        wait(dve, shifted, i, TT, t - 1)
                    dve.sem_inc(own_wait, 1)
                    for h in range(8 * b, 8 * b + 8):
                        last = dve.max(v8[:, t % 2, h, :], Lb[:, t % 2, h, 0:NL])
                    if b:
                        last.then_inc(top8, 1)

                def slots(t):
                    wait(dve, top8, i, TT, t + 1)
                    dve.memset(v8[:, t % 2, :, TOPK:8], PAD).then_inc(v8_ready, 1)
                    wait(dve, recip_ready, i, TT, t - 1)
                    dve.tensor_tensor(d4[:, t % 2, :, :], v8[:, t % 2, :, 0:TOPK],
                                      v8[:, t % 2, :, 0:1].broadcast_to([P, H, TOPK]), ALU.subtract).then_inc(d4_ready, 1)

                def replace(t, b):
                    wait(dve, v8_ready, i, TT, t + 1)
                    wait(dve, p_raw, i, TT, t)
                    if ffn and t == 0 and b == 0:
                        for o in (2, 3):
                            wait(dve, out_stored[o], j, 16, 0)
                    dve.sem_inc(own_wait, 1)
                    for h in range(8 * b, 8 * b + 8):
                        last = dve.match_replace(Lr[:, h, :], v8[:, t % 2, h, :], Lb[:, t % 2, h, :], HIT)
                    if b:
                        last.then_inc(replaced, 1)

                def sums(t):
                    wait(dve, e4_ready, i, TT, t + 1)
                    dve.tensor_reduce(s4[:, t % 2, :], d4[:, t % 2, :, :], AX.X, ALU.add).then_inc(sum_ready, 1)
                    wait(dve, sum_ready, i, TT, t + 1)
                    wait(dve, p_ready, i, TT, t - 1)
                    dve.reciprocal(r4[:, t % 2, :], s4[:, t % 2, :]).then_inc(recip_ready, 1)

                def select(t):
                    wait(dve, e_ready, i, TT, t + 1)
                    buf = Lb[:, t % 2, :, 0:NL]
                    dve.scalar_tensor_tensor(out=buf, in0=Lr[:, :, 0:NL], scalar=HIT, in1=buf,
                                             op0=ALU.is_equal, op1=ALU.mult).then_inc(p_raw, 1)

                def probs_lo(t):
                    wait(dve, p_hi, i, TT, t + 1)
                    dve.scalar_tensor_tensor(out=halves[:, 1, :], in0=Pb, scalar=PS, in1=halves[:, 0, :],
                                             op0=ALU.mult, op1=ALU.subtract).then_inc(p_lo, 1)

                def f_a(t):
                    s = t % 2
                    wait(dve, dn_done, j, TT, t + 1)
                    dve.bn_stats(stf[:, s, :], ring[:, plan[("DN", -1, t)][0], :]).then_inc(f_stats, 1)
                    wait(dve, f_stats, j, TT, t + 1)
                    dve.sem_inc(own_wait, 1)
                    dve.bn_aggr(mvf[:, s, :], stf[:, s, :]).then_inc(f_mean, 1)
                    wait(dve, f_mean, j, TT, t + 1)
                    dve.tensor_scalar(vaf[:, s:s + 1], mvf[:, s, 1:2], cf[:, 1:2], cf[:, 1:2], ALU.mult, ALU.mult).then_inc(f_varc, 1)
                    wait(dve, f_varc, j, TT, t + 1)
                    dve.tensor_scalar(vaf[:, s:s + 1], vaf[:, s:s + 1], EPS, None, ALU.add).then_inc(f_var, 1)

                def f_b(t):
                    s = t % 2
                    wait(dve, f_rstd, j, TT, t + 1)
                    wait(dve, out_ready, j, TT, t - 1)
                    dve.tensor_tensor(rcf[:, s:s + 1], rsf[:, s:s + 1], cf[:, 1:2], ALU.mult).then_inc(f_scale, 1)
                    wait(dve, f_scale, j, TT, t + 1)
                    dve.scalar_tensor_tensor(out=nbf[:, s:s + 1], in0=mvf[:, s, 0:1], scalar=rcf[:, s:s + 1],
                                             in1=(nby_last if kind == "tail" else nby)[:, t:t + 1],
                                             op0=ALU.mult, op1=ALU.subtract, reverse1=True).then_inc(f_bias, 1)
                    wait(dve, out_stored[(t + 2) % 4], j, 16, 16 if t >= 2 else 0)
                    dve.scalar_tensor_tensor(out=out_buf[s], in0=ring[:, plan[("DN", -1, t)][0], :], scalar=rcf[:, s:s + 1],
                                             in1=residual(kind == "tail")[:, t, :], op0=ALU.mult, op1=ALU.add).then_inc(f_sum, 1)

                def y_a(t):
                    s = t % 2
                    wait(dve, wo_done, i, TT, t + 1)
                    if kind == "first" and t == 0:
                        dve.wait_ge(aw_loaded[6], 16)
                        dve.wait_ge(lat_lo, 2)
                    wait(dve, x1_ready, i, TT, t - 1)
                    dve.scalar_tensor_tensor(out=row[:, s, :], in0=ring[:, plan[("WO", 0, t)][0], :], scalar=clo[:, 1:2],
                                             in1=bo_b[:, :], op0=ALU.mult, op1=ALU.add).then_inc(y_ready, 1)
                    wait(dve, y_ready, i, TT, t + 1)
                    dve.bn_stats(sty[:, s, :], row[:, s, :]).then_inc(y_stats, 1)
                    wait(dve, y_stats, i, TT, t + 1)
                    dve.sem_inc(own_wait, 1)
                    dve.bn_aggr(mvy[:, s, :], sty[:, s, :]).then_inc(y_mean, 1)
                    wait(dve, y_mean, i, TT, t + 1)
                    dve.tensor_scalar(vay[:, s:s + 1], mvy[:, s, 1:2], EPS, None, ALU.add).then_inc(y_var, 1)

                def y_b(t):
                    s = t % 2
                    wait(dve, y_rstd, i, TT, t + 1)
                    if kind == "last":
                        wait(dve, xn1_ready, i, TT, TT)
                    else:
                        wait(dve, x_res_loaded[t], i, 16, 16)
                    buf = residual(kind == "last")[:, t, :]
                    dve.scalar_tensor_tensor(out=buf, in0=row[:, s, :], scalar=rsy[:, s:s + 1], in1=buf, op0=ALU.mult, op1=ALU.add).then_inc(x1_ready, 1)
                    dve.tensor_scalar((nby_last if kind == "last" else nby)[:, t:t + 1], mvy[:, s, 0:1], rsy[:, s:s + 1], -1.0, ALU.mult, ALU.mult)
                    wait(dve, x1_ready, i, TT, t + 1)
                    dve.bn_stats(stx[:, s, :], buf).then_inc(ln2_stats, 1)
                    wait(dve, ln2_stats, i, TT, t + 1)
                    dve.sem_inc(own_wait, 1)
                    dve.bn_aggr(mvx[:, s, :], stx[:, s, :]).then_inc(ln2_mean, 1)
                    wait(dve, ln2_mean, i, TT, t + 1)
                    dve.tensor_scalar(vax[:, s:s + 1], mvx[:, s, 1:2], XS ** -2, EPS * XS ** -2, ALU.mult, ALU.add).then_inc(ln2_var, 1)

                def y_c(c, t):
                    s = t % 2
                    wait(dve, ln2_rstd, i + c, TT, t + 1)
                    wait(dve, xn2_ready, i + c, TT, t - 1)
                    dve.tensor_scalar(nbx[:, s:s + 1], mvx[:, s, 0:1], rsx[:, s:s + 1], -1.0, ALU.mult, ALU.mult).then_inc(ln2_bias, 1)

                if kind == "first":
                    ln1_stat(0)
                    maxima(latr, 3, 32, 2)
                    maxima(bqc[:, :], 4, 16, 1)
                    ln1_biases(0)
                    maxima(raw_a[0], 0, 16, 0)
                    dve.wait_ge(mx_ready, 3)
                    dve.tensor_copy(mg[:, 1:2], mx[:, 2:3])
                    dve.tensor_tensor(mg[:, 0:1], mx[:, 0:1], mx[:, 1:2], ALU.max).then_inc(mg_ready, 1)
                    dve.wait_ge(idents, 1)
                    dve.tensor_copy(id16[:, :], id32[:, :]).then_inc(idents, 1)
                    powers(0)
                    for t in range(TT):
                        s1_lo(0, t)
                    weights_lo(0)
                    latL_lo()
                    for n in ASUM_DVE:
                        abs_sum(n)
                    tern_total(0)
                    tern_scale_of(0)
                    ternarise(0)
                    maxima(bvc[:, :], 5, 16, 4)
                    maxima(raw_a[1], 1, 16, 3)
                    ternarise(1)
                    maxima(raw_a[2], 2, 16, 5)
                    dve.wait_ge(mx_ready, 6)
                    dve.tensor_copy(mg[:, 3:4], mx[:, 5:6])
                    dve.tensor_reduce(mg[:, 2:3], mx[:, 2:5], AX.X, ALU.max).then_inc(mg_ready, 1)
                    low_q()
                    powers(1)
                    ternarise(2)
                if ffn and att:
                    y_c(-1, 3)
                    t2_lo(-1, 3)
                    low_q()
                if kind == "first":
                    ternarise(3)
                    after = {0: [(maxes, 0, 0), (maxes, 0, 1), (slots, 0), (replace, 0, 0), (replace, 0, 1), (weights_lo, 1)],
                             2: [(maxes, 1, 0), (sums, 0), (select, 0)], 3: [(maxes, 1, 1), (slots, 1)],
                             4: [(tern_total, 1), (replace, 1, 0), (replace, 1, 1), (tern_scale_of, 1)],
                             5: [(weights_lo, 2), (latV_lo,)],
                             6: [(probs_lo, 0), (maxes, 2, 0), (maxes, 2, 1), (sums, 1), (select, 1), (slots, 2)],
                             7: [(replace, 2, 0), (replace, 2, 1)],
                             9: [(probs_lo, 1), (maxes, 3, 0), (maxes, 3, 1), (sums, 2), (select, 2), (slots, 3)],
                             10: [(replace, 3, 0), (replace, 3, 1)], 11: [(tern_total, 2)], 12: [(probs_lo, 2), (sums, 3), (select, 3), (tern_scale_of, 2)],
                             13: [(probs_lo, 3)], 15: [(ln1_stat, 1)], 16: [(ln1_biases, 1)],
                             18: [(s1_lo, 1, 0)], 20: [(s1_lo, 1, 1)], 22: [(s1_lo, 1, 2)],
                             23: [(s1_lo, 1, 3), (y_a, 0), (y_a, 1), (y_b, 0), (y_b, 1), (y_c, 0, 0), (y_a, 2), (y_c, 0, 1), (t2_lo, 0, 0)]}
                    for n in range(24):
                        if n and n + AHEAD < 24:
                            ternarise(n + AHEAD)
                        for f, *a in after.get(n, ()):
                            f(*a)
                    y_a(3)
                    t2_lo(0, 1)
                    y_b(2)
                    y_b(3)
                    y_c(0, 2)
                    t2_lo(0, 2)
                    ffn_scales()
                    return
                AFTER = {0: [(maxes, 0, 0)], 1: [(maxes, 0, 1), (slots, 0), (replace, 0, 0)],
                         2: [(replace, 0, 1), (maxes, 1, 0)], 3: [(sums, 0), (select, 0), (maxes, 1, 1), (slots, 1)],
                         4: [(replace, 1, 0)], 5: [(replace, 1, 1), (probs_lo, 0)],
                         6: [(sums, 1), (select, 1), (maxes, 2, 0)], 7: [(maxes, 2, 1), (slots, 2)],
                         8: [(replace, 2, 0)], 9: [(replace, 2, 1), (probs_lo, 1)],
                         10: [(sums, 2), (select, 2)], 11: [(maxes, 3, 0), (maxes, 3, 1), (slots, 3)],
                         12: [(replace, 3, 0)], 13: [(replace, 3, 1), (probs_lo, 2)],
                         14: [(sums, 3), (select, 3)], 15: []}
                for e in range(NE):
                    if ffn:
                        hidden(e)
                    if att:
                        for f, *a in AFTER[e]:
                            f(*a)
                if att:
                    probs_lo(3)
                if nxt:
                    ln1_stat(1)
                    ln1_biases(1)
                if ffn:
                    f_a(0)
                    f_b(0)
                if nxt:
                    s1_lo(1, 0)
                    s1_lo(1, 1)
                if ffn:
                    f_a(1)
                    f_b(1)
                if nxt:
                    s1_lo(1, 2)
                    s1_lo(1, 3)
                if nxt:
                    f_a(2)
                    f_b(2)
                if att:
                    y_a(0)
                    y_a(1)
                    y_b(0)
                    y_b(1)
                    y_c(0, 0)
                    y_a(2)
                    y_c(0, 1)
                    t2_lo(0, 0)
                if nxt:
                    f_a(3)
                    t2_lo(0, 1)
                    f_b(3)
                    y_b(2)
                    y_a(3)
                    y_c(0, 2)
                    y_b(3)
                    t2_lo(0, 2)
                if kind == "last":
                    y_a(3)
                    t2_lo(0, 1)
                    y_b(2)
                    y_b(3)
                    y_c(0, 2)
                    t2_lo(0, 2)
                    y_c(0, 3)
                    t2_lo(0, 3)
                if not nxt:
                    for t in (2, 3):
                        f_a(t)
                        f_b(t)

            bodies(dve, body)


_INS = ["L0_attn_hidden_states", "L0_attn_Wq", "L0_attn_bq", "L0_attn_Wv", "L0_attn_bv", "L0_attn_Wo", "L0_attn_bo",
        "L0_attn_latent_keys", "L0_ffn_W_up", "L0_ffn_W_gate", "L0_ffn_W_down"]


def kernel(**inputs):
    import numpy as _np
    import concourse.bacc as _bacc
    from concourse import mybir as _mybir
    from concourse.bass_utils import run_bass_kernel_spmd as _run

    nc = _bacc.Bacc("TRN2", target_bir_lowering=False, num_devices=1)
    arrays, args = {}, []
    for name in _INS:
        a = _np.ascontiguousarray(inputs[name])
        arrays[f"in_{name}"] = a
        args.append(nc.dram_tensor(f"in_{name}", a.shape, _mybir.dt.from_np(a.dtype), kind="ExternalInput").ap())
    shape = inputs["L0_attn_hidden_states"].shape
    o = nc.dram_tensor("out_dram", shape, _mybir.dt.float32, kind="ExternalOutput").ap()
    build(nc, *args, o)
    r = _run(nc, [arrays], core_ids=[0])
    return r.results[0]["out_dram"]
```
